# Optimizing a Trainium2 kernel written in Bass

```python
import numpy as np
import jax
import jax.numpy as jnp

def _softmax(x, axis=-1):
    return jax.nn.softmax(x, axis=axis)

def _gelu(x):
    return jax.nn.gelu(x, approximate=True)

def _silu(x):
    return jax.nn.silu(x)

def _sigmoid(x):
    return jax.nn.sigmoid(x)

def _layernorm(x, axis=-1, eps=1e-05):
    m = jnp.mean(x, axis=axis, keepdims=True)
    v = jnp.var(x, axis=axis, keepdims=True)
    return (x - m) / jnp.sqrt(v + eps)

def _scatter_add(tgt, idx, src, axis=0):
    return tgt.at[idx].add(src)

def _segment_sum(src, seg, n):
    return jax.ops.segment_sum(src, seg, n)
kernel_name = 'mk_adaln_attn_ffn_d1_seqx_r8_3a2bba'

def setup_inputs(seed: int=0):
    np.random.seed(seed)
    _w = jnp.asarray

    def _rec_inputs():
        import jax
        import jax.numpy as jnp
        _rk = jax.random.key(seed)
        x = -0.000125 + 0.9999 * jax.random.normal(jax.random.fold_in(_rk, 1), (4, 256, 256), jnp.float32)
        _lenS = 256 - jax.random.randint(jax.random.fold_in(_rk, 7), (4,), 0, max(1, 256 // 4) + 1, jnp.int32)
        _lenS2 = 256 - jax.random.randint(jax.random.fold_in(_rk, 8), (4,), 0, max(1, 256 // 4) + 1, jnp.int32)
        fside_BxSxS_0 = -1.52775e-05 + 0.999936 * jax.random.normal(jax.random.fold_in(_rk, 11), (4, 256, 256), jnp.float32)
        cond_512 = -5.03954e-05 + 1.00559 * jax.random.normal(jax.random.fold_in(_rk, 12), (4, 64), jnp.float32)
        return (x, fside_BxSxS_0, cond_512)
    x, fside_BxSxS_0, cond_512 = _rec_inputs()

    def _L0_cond_setup():
        import jax, jax.numpy as jnp
        from jax import lax
        import numpy as np
        B, T, C, TD = (8, 256, 256, 64)

        def _bi_wkv(r, k, v, w, u, time_emb):
            tf = jax.nn.sigmoid(jnp.sum(time_emb, axis=-1))[:, None, None]
            decay = jnp.exp(-jnp.exp(w.astype(jnp.float32)))[None, :] * (0.5 + 0.5 * tf[:, :, 0])
            kf = k.astype(jnp.float32)
            vf = v.astype(jnp.float32)
            ek = jnp.exp(jnp.minimum(kf, 30.0))
            ekv = ek * vf

            def step(carry, x):
                a, b = carry
                ekv_t, ek_t = x
                a = a * decay + ekv_t
                b = b * decay + ek_t
                return ((a, b), (a, b))
            ekv_t = jnp.swapaxes(ekv, 0, 1)
            ek_t = jnp.swapaxes(ek, 0, 1)
            init = (jnp.zeros_like(decay), jnp.zeros_like(decay))
            _, (nf, df) = lax.scan(step, init, (ekv_t, ek_t))
            _, (nb, db) = lax.scan(step, init, (ekv_t, ek_t), reverse=True)
            nf = jnp.swapaxes(nf, 0, 1)
            df = jnp.swapaxes(df, 0, 1)
            nb = jnp.swapaxes(nb, 0, 1)
            db = jnp.swapaxes(db, 0, 1)
            euk = jnp.exp(jnp.minimum(u.astype(jnp.float32)[None, None, :] + kf, 30.0))
            num = nf + nb - ekv + euk * vf
            den = df + db - ek + euk
            base = jax.nn.sigmoid(r.astype(jnp.float32)) * (num / jnp.maximum(den, 1e-08))
            out = base * (0.8 + 0.2 * tf)
            return out.astype(r.dtype)
        key = jax.random.key(seed)
        ks = jax.random.split(key, 6)
        return {'r': jax.random.normal(ks[0], (B, T, C), dtype=jnp.float32), 'k': jax.random.normal(ks[1], (B, T, C), dtype=jnp.float32), 'v': jax.random.normal(ks[2], (B, T, C), dtype=jnp.float32), 'w': jax.random.normal(ks[3], (C,), dtype=jnp.float32), 'u': jax.random.normal(ks[4], (C,), dtype=jnp.float32), 'time_emb': jax.random.normal(ks[5], (B, TD), dtype=jnp.float32)}
    _L0_cond_all = _L0_cond_setup()
    _L0_cond_in = {k: v for k, v in _L0_cond_all.items() if k in ('w', 'u')}
    del _L0_cond_all

    def _L0_attn_setup():
        import jax, jax.numpy as jnp
        import numpy as np
        B, S, E, H = (2, 256, 256, 16)
        HD = E // H
        key = jax.random.key(seed)
        ks = jax.random.split(key, 7)
        inp = {'query': jax.random.normal(ks[0], (B, S, E), dtype=jnp.float32), 'key': jax.random.normal(ks[1], (B, S, E), dtype=jnp.float32), 'value': jax.random.normal(ks[2], (B, S, E), dtype=jnp.float32), 'Wqkv': jax.random.normal(ks[3], (3 * E, E), dtype=jnp.float32) * E ** (-0.5), 'bqkv': jnp.zeros((3 * E,), dtype=jnp.float32), 'Wproj': jax.random.normal(ks[4], (E, E), dtype=jnp.float32) * E ** (-0.5), 'bproj': jnp.zeros((E,), dtype=jnp.float32)}
        return inp
    _L0_attn_all = _L0_attn_setup()
    _L0_attn_in = {k: v for k, v in _L0_attn_all.items() if k in ('key', 'value', 'Wqkv', 'bqkv', 'Wproj', 'bproj')}
    del _L0_attn_all

    def _L0_cond2_setup():
        import jax, jax.numpy as jnp
        from jax import lax
        import numpy as np
        B, T, C, TD = (8, 256, 256, 64)

        def _bi_wkv(r, k, v, w, u, time_emb):
            tf = jax.nn.sigmoid(jnp.sum(time_emb, axis=-1))[:, None, None]
            decay = jnp.exp(-jnp.exp(w.astype(jnp.float32)))[None, :] * (0.5 + 0.5 * tf[:, :, 0])
            kf = k.astype(jnp.float32)
            vf = v.astype(jnp.float32)
            ek = jnp.exp(jnp.minimum(kf, 30.0))
            ekv = ek * vf

            def step(carry, x):
                a, b = carry
                ekv_t, ek_t = x
                a = a * decay + ekv_t
                b = b * decay + ek_t
                return ((a, b), (a, b))
            ekv_t = jnp.swapaxes(ekv, 0, 1)
            ek_t = jnp.swapaxes(ek, 0, 1)
            init = (jnp.zeros_like(decay), jnp.zeros_like(decay))
            _, (nf, df) = lax.scan(step, init, (ekv_t, ek_t))
            _, (nb, db) = lax.scan(step, init, (ekv_t, ek_t), reverse=True)
            nf = jnp.swapaxes(nf, 0, 1)
            df = jnp.swapaxes(df, 0, 1)
            nb = jnp.swapaxes(nb, 0, 1)
            db = jnp.swapaxes(db, 0, 1)
            euk = jnp.exp(jnp.minimum(u.astype(jnp.float32)[None, None, :] + kf, 30.0))
            num = nf + nb - ekv + euk * vf
            den = df + db - ek + euk
            base = jax.nn.sigmoid(r.astype(jnp.float32)) * (num / jnp.maximum(den, 1e-08))
            out = base * (0.8 + 0.2 * tf)
            return out.astype(r.dtype)
        key = jax.random.key(seed)
        ks = jax.random.split(key, 6)
        return {'r': jax.random.normal(ks[0], (B, T, C), dtype=jnp.float32), 'k': jax.random.normal(ks[1], (B, T, C), dtype=jnp.float32), 'v': jax.random.normal(ks[2], (B, T, C), dtype=jnp.float32), 'w': jax.random.normal(ks[3], (C,), dtype=jnp.float32), 'u': jax.random.normal(ks[4], (C,), dtype=jnp.float32), 'time_emb': jax.random.normal(ks[5], (B, TD), dtype=jnp.float32)}
    _L0_cond2_all = _L0_cond2_setup()
    _L0_cond2_in = {k: v for k, v in _L0_cond2_all.items() if k in ('w', 'u')}
    del _L0_cond2_all

    def _L0_ffn_setup():
        import jax, jax.numpy as jnp
        import numpy as np
        B, S, H = (2, 64, 256)
        E, G, TOPK_G, K = (64, 8, 4, 6)
        I = 64
        SH_I = 256
        RSF = 2.5

        def relu2(x):
            r = jax.nn.relu(x)
            return r * r
        key = jax.random.key(seed)
        ks = jax.random.split(key, 7)
        s = lambda d: 1.0 / np.sqrt(d)
        return {'hidden_states': jax.random.normal(ks[0], (B, S, H), jnp.float32), 'gate_w': jax.random.normal(ks[1], (E, H), jnp.float32) * s(H), 'gate_bias': jax.random.normal(ks[2], (E,), jnp.float32) * 0.01, 'w1': jax.random.normal(ks[3], (E, I, H), jnp.float32) * s(H), 'w2': jax.random.normal(ks[4], (E, H, I), jnp.float32) * s(I), 'shared_up': jax.random.normal(ks[5], (SH_I, H), jnp.float32) * s(H), 'shared_down': jax.random.normal(ks[6], (H, SH_I), jnp.float32) * s(SH_I)}
    _L0_ffn_all = _L0_ffn_setup()
    _L0_ffn_in = {k: v for k, v in _L0_ffn_all.items() if k in ('gate_w', 'gate_bias', 'w1', 'w2', 'shared_up', 'shared_down')}
    del _L0_ffn_all
    return {'x': x, 'fside_BxSxS_0': fside_BxSxS_0, 'cond_512': cond_512, 'L0_cond_w': _L0_cond_in['w'], 'L0_cond_u': _L0_cond_in['u'], 'L0_attn_key': _L0_attn_in['key'], 'L0_attn_value': _L0_attn_in['value'], 'L0_attn_Wqkv': _L0_attn_in['Wqkv'], 'L0_attn_bqkv': _L0_attn_in['bqkv'], 'L0_attn_Wproj': _L0_attn_in['Wproj'], 'L0_attn_bproj': _L0_attn_in['bproj'], 'L0_cond2_w': _L0_cond2_in['w'], 'L0_cond2_u': _L0_cond2_in['u'], 'L0_ffn_gate_w': _L0_ffn_in['gate_w'], 'L0_ffn_gate_bias': _L0_ffn_in['gate_bias'], 'L0_ffn_w1': _L0_ffn_in['w1'], 'L0_ffn_w2': _L0_ffn_in['w2'], 'L0_ffn_shared_up': _L0_ffn_in['shared_up'], 'L0_ffn_shared_down': _L0_ffn_in['shared_down']}

def reference(x, fside_BxSxS_0, cond_512, L0_cond_w, L0_cond_u, L0_attn_key, L0_attn_value, L0_attn_Wqkv, L0_attn_bqkv, L0_attn_Wproj, L0_attn_bproj, L0_cond2_w, L0_cond2_u, L0_ffn_gate_w, L0_ffn_gate_bias, L0_ffn_w1, L0_ffn_w2, L0_ffn_shared_up, L0_ffn_shared_down):
    import jax
    import jax.numpy as jnp

    def _L0_cond_ref(r, k, v, w, u, time_emb):
        import jax, jax.numpy as jnp
        from jax import lax
        import numpy as np
        B, T, C, TD = (8, 256, 256, 64)

        def _bi_wkv(r, k, v, w, u, time_emb):
            tf = jax.nn.sigmoid(jnp.sum(time_emb, axis=-1))[:, None, None]
            decay = jnp.exp(-jnp.exp(w.astype(jnp.float32)))[None, :] * (0.5 + 0.5 * tf[:, :, 0])
            kf = k.astype(jnp.float32)
            vf = v.astype(jnp.float32)
            ek = jnp.exp(jnp.minimum(kf, 30.0))
            ekv = ek * vf

            def step(carry, x):
                a, b = carry
                ekv_t, ek_t = x
                a = a * decay + ekv_t
                b = b * decay + ek_t
                return ((a, b), (a, b))
            ekv_t = jnp.swapaxes(ekv, 0, 1)
            ek_t = jnp.swapaxes(ek, 0, 1)
            init = (jnp.zeros_like(decay), jnp.zeros_like(decay))
            _, (nf, df) = lax.scan(step, init, (ekv_t, ek_t))
            _, (nb, db) = lax.scan(step, init, (ekv_t, ek_t), reverse=True)
            nf = jnp.swapaxes(nf, 0, 1)
            df = jnp.swapaxes(df, 0, 1)
            nb = jnp.swapaxes(nb, 0, 1)
            db = jnp.swapaxes(db, 0, 1)
            euk = jnp.exp(jnp.minimum(u.astype(jnp.float32)[None, None, :] + kf, 30.0))
            num = nf + nb - ekv + euk * vf
            den = df + db - ek + euk
            base = jax.nn.sigmoid(r.astype(jnp.float32)) * (num / jnp.maximum(den, 1e-08))
            out = base * (0.8 + 0.2 * tf)
            return out.astype(r.dtype)
        return _bi_wkv(r, k, v, w, u, time_emb)

    def _L0_attn_ref(query, key, value, Wqkv, bqkv, Wproj, bproj):
        import jax, jax.numpy as jnp
        import numpy as np
        B, S, E, H = (2, 256, 256, 16)
        HD = E // H
        b, s, _ = query.shape
        qkv = query @ Wqkv.T + bqkv
        qkv = qkv.reshape(b, s, H, 3 * HD).transpose(0, 2, 1, 3)
        q = qkv[..., :HD]
        k = qkv[..., HD:2 * HD]
        v = qkv[..., 2 * HD:]
        scores = jnp.einsum('bhqd,bhkd->bhqk', q, k) * HD ** 0.5
        attn = jax.nn.softmax(scores, axis=-1)
        out = jnp.einsum('bhqk,bhkd->bhqd', attn, v)
        out = out.transpose(0, 2, 1, 3).reshape(b, s, E)
        return out @ Wproj.T + bproj

    def _L0_cond2_ref(r, k, v, w, u, time_emb):
        import jax, jax.numpy as jnp
        from jax import lax
        import numpy as np
        B, T, C, TD = (8, 256, 256, 64)

        def _bi_wkv(r, k, v, w, u, time_emb):
            tf = jax.nn.sigmoid(jnp.sum(time_emb, axis=-1))[:, None, None]
            decay = jnp.exp(-jnp.exp(w.astype(jnp.float32)))[None, :] * (0.5 + 0.5 * tf[:, :, 0])
            kf = k.astype(jnp.float32)
            vf = v.astype(jnp.float32)
            ek = jnp.exp(jnp.minimum(kf, 30.0))
            ekv = ek * vf

            def step(carry, x):
                a, b = carry
                ekv_t, ek_t = x
                a = a * decay + ekv_t
                b = b * decay + ek_t
                return ((a, b), (a, b))
            ekv_t = jnp.swapaxes(ekv, 0, 1)
            ek_t = jnp.swapaxes(ek, 0, 1)
            init = (jnp.zeros_like(decay), jnp.zeros_like(decay))
            _, (nf, df) = lax.scan(step, init, (ekv_t, ek_t))
            _, (nb, db) = lax.scan(step, init, (ekv_t, ek_t), reverse=True)
            nf = jnp.swapaxes(nf, 0, 1)
            df = jnp.swapaxes(df, 0, 1)
            nb = jnp.swapaxes(nb, 0, 1)
            db = jnp.swapaxes(db, 0, 1)
            euk = jnp.exp(jnp.minimum(u.astype(jnp.float32)[None, None, :] + kf, 30.0))
            num = nf + nb - ekv + euk * vf
            den = df + db - ek + euk
            base = jax.nn.sigmoid(r.astype(jnp.float32)) * (num / jnp.maximum(den, 1e-08))
            out = base * (0.8 + 0.2 * tf)
            return out.astype(r.dtype)
        return _bi_wkv(r, k, v, w, u, time_emb)

    def _L0_ffn_ref(hidden_states, gate_w, gate_bias, w1, w2, shared_up, shared_down):
        import jax, jax.numpy as jnp
        import numpy as np
        B, S, H = (2, 64, 256)
        E, G, TOPK_G, K = (64, 8, 4, 6)
        I = 64
        SH_I = 256
        RSF = 2.5

        def relu2(x):
            r = jax.nn.relu(x)
            return r * r
        x = hidden_states.reshape(-1, H)
        T = x.shape[0]
        logits = jnp.dot(x.astype(jnp.float32), gate_w.astype(jnp.float32).T)
        scores = jax.nn.sigmoid(logits)
        scores_b = scores + gate_bias
        sb_g = scores_b.reshape(T, G, E // G)
        group_scores = jnp.sum(jax.lax.top_k(sb_g, 2)[0], axis=-1)
        grp_idx = jax.lax.top_k(group_scores, TOPK_G)[1]
        grp_mask = jnp.sum(jax.nn.one_hot(grp_idx, G, dtype=jnp.float32), axis=1)
        expert_mask = jnp.repeat(grp_mask, E // G, axis=-1) > 0
        masked = jnp.where(expert_mask, scores_b, -jnp.inf)
        _, top_idx = jax.lax.top_k(masked, K)
        topw = jnp.take_along_axis(scores, top_idx, axis=1)
        topw = topw / (jnp.sum(topw, axis=-1, keepdims=True) + 1e-20) * RSF
        w_dense = jnp.zeros((T, E), jnp.float32).at[jnp.arange(T)[:, None], top_idx].add(topw)
        h = relu2(jnp.einsum('th,eih->tei', x, w1))
        h = h * w_dense[:, :, None]
        routed = jnp.einsum('tei,ehi->th', h, w2)
        shared = jnp.dot(relu2(jnp.dot(x, shared_up.T)), shared_down.T)
        out = (routed + shared).astype(hidden_states.dtype)
        return out.reshape(hidden_states.shape)
    x = x + _L0_attn_ref(_L0_cond_ref(x, fside_BxSxS_0, fside_BxSxS_0, L0_cond_w, L0_cond_u, cond_512), L0_attn_key, L0_attn_value, L0_attn_Wqkv, L0_attn_bqkv, L0_attn_Wproj, L0_attn_bproj)
    x = x + _L0_ffn_ref(_L0_cond2_ref(x, fside_BxSxS_0, fside_BxSxS_0, L0_cond2_w, L0_cond2_u, cond_512), L0_ffn_gate_w, L0_ffn_gate_bias, L0_ffn_w1, L0_ffn_w2, L0_ffn_shared_up, L0_ffn_shared_down)
    return x

_drawn_inputs = setup_inputs


def setup_inputs(seed=0):
    import zlib

    import numpy as np

    out = dict(_drawn_inputs(seed))
    spreads = {'L0_attn_bqkv': (0.0, 0.1), 'L0_attn_bproj': (0.0, 0.1)}
    factors = {}
    for name, (base, spread) in spreads.items():
        noise = np.random.default_rng([zlib.crc32(name.encode()), seed]).standard_normal(out[name].shape)
        drawn = base * np.exp(spread * noise) if base else spread * noise
        out[name] = jnp.asarray(drawn.astype(out[name].dtype))
    for name, factor in factors.items():
        out[name] = (out[name] * factor).astype(out[name].dtype)
    return out
```

```python
from contextlib import ExitStack

import concourse.bass as bass
from concourse import mybir

P = 128
B, S, C = 4, 256, 256
TOK = B * S
KC = C // P
H, HD = 16, 16
HB = H // KC
QT = S // P
E, I = 64, 64
G, GT, TOPK = 8, 4, 6
EG = E // G
TILES = E * I // P
SHARED = 256 // P
NT = TILES + SHARED
TD = 64
ROLE = 4
STACK = ROLE * HD
MAXROW = 96
HT = 512
SCALE = float(HD) ** 0.5
PRING = 6
BIG = 1.0e30
NONE = -3.0e38

F32 = mybir.dt.float32
F32R = mybir.dt.float32r
I32 = mybir.dt.int32
ALU = mybir.AluOpType
ACT = mybir.ActivationFunctionType
AX_X = mybir.AxisListType.X

V_W1, V_U1, V_W2, V_U2, V_BQ, V_BK, V_BP = (KC * n for n in range(7))
NVEC = 7 * KC


def bass_adaln_attn_ffn(nc, xT, fT, cond, vecs, w_in, w_out, gate_w, bv, gate_bias, tiles, out):
    qk_dram = nc.dram_tensor("qk_split", (4, C, TOK), F32, kind="Internal").ap()

    with ExitStack() as ctx:
        def sb(name, shape, dt=F32):
            return ctx.enter_context(nc.sbuf_tensor(name, shape, dt))

        def sem(name):
            return ctx.enter_context(nc.semaphore(name))

        ps = ctx.enter_context(nc.psum_tensor("ps", [P, 8, 512], F32))

        x_sb = sb("x_sb", [P, KC, TOK])
        f_sb = sb("f_sb", [P, KC, TOK])
        vec = sb("vec", [P, NVEC])
        cond_sb = sb("cond_sb", [P, B, TD])
        wi = sb("wi", [P, KC, 3 * C])
        wo = sb("wo", [P, KC, C])
        gw = sb("gw", [P, KC, E])
        bvb = sb("bvb", [P, C])
        gbb = sb("gbb", [P, E])
        ident = sb("ident", [P, P])
        selval = sb("selval", [P, P])
        sel_i = sb("sel_i", [P, P], I32)
        tile_i = sb("tile_i", [P, TILES], I32)
        tile_no = sb("tile_no", [P, TILES])
        tsum = sb("tsum", [P, B])
        tex = sb("tex", [P, B])
        tden = sb("tden", [P, B])
        tf = sb("tf", [P, B])
        thalf = sb("thalf", [P, B])
        cfac = sb("cfac", [P, B])
        dexp = sb("dexp", [P, 2 * KC])
        dbase = sb("dbase", [P, 2 * KC])
        decay = sb("decay", [P, 2 * KC, B])
        clip = sb("clip", [P, 4, KC, S])
        ex = sb("ex", [P, 4, KC, S])
        ekv = sb("ekv", [P, KC, S])
        gk = sb("gk", [P, 2, KC, S])
        gkv = sb("gkv", [P, 2, KC, S])
        scan = sb("scan", [P, 8, KC, S])
        num = sb("num", [P, 2, 2, KC, S])
        den = sb("den", [P, 2, 2, KC, S])
        lnd = sb("lnd", [P, KC, S])
        lne = sb("lne", [P, KC, S])
        hid1 = sb("hid1", [P, KC, S])
        qk_hi = sb("qk_hi", [P, 2, KC, S], F32R)
        qk_lo = sb("qk_lo", [P, 2, KC, S], F32R)
        v_aug = sb("v_aug", [P, 2, QT, H, 32])
        q_st = sb("q_st", [P, H, S], F32R)
        k_st = sb("k_st", [P, H, S], F32R)
        mx = sb("mx", [P, 2, H, QT])
        nmax_hi = sb("nmax_hi", [H, KC, P], F32R)
        nmax_lo = sb("nmax_lo", [H, KC, P], F32R)
        prob = sb("prob", [P, PRING, QT, S])
        o_raw = sb("o_raw", [P, 4, S])
        rsum = sb("rsum", [P, QT, H])
        o_tok = sb("o_tok", [P, QT, H, HD])
        o_ch = sb("o_ch", [P, KC, S])
        x1 = sb("x1", [P, KC, TOK])
        clip2 = sb("clip2", [P, KC, S])
        ex2 = sb("ex2", [P, KC, S])
        lne2 = ex2
        lnd2 = sb("lnd2", [P, KC, S])
        hid2 = sb("hid2", [P, KC, S])
        hid_hi = sb("hid_hi", [P, KC, TOK], F32R)
        hid_lo = sb("hid_lo", [P, KC, TOK], F32R)
        gex = sb("gex", [P, QT, E])
        gden = sb("gden", [P, QT, E])
        score = sb("score", [P, QT, E])
        sbias = sb("sbias", [P, QT, G, EG])
        pmax = sb("pmax", [P, QT * G, 4])
        pmin = sb("pmin", [P, QT * G, 4])
        qmax = sb("qmax", [P, QT * G, 2])
        qmid = sb("qmid", [P, QT * G, 2])
        qlow = sb("qlow", [P, QT * G, 2])
        qsec = sb("qsec", [P, QT * G, 2])
        fmax = sb("fmax", [P, QT * G, 1])
        fmid = sb("fmid", [P, QT * G, 1])
        flow = sb("flow", [P, QT * G, 1])
        fsec = sb("fsec", [P, QT * G, 1])
        gsum = sb("gsum", [P, QT, G + 4])
        gtop = sb("gtop", [P, QT, 8])
        grep = sb("grep", [P, QT, G + 4])
        gpen = sb("gpen", [P, QT, G])
        masked = sb("masked", [P, QT, E + 2])
        etop = sb("etop", [P, QT, 8])
        erep = sb("erep", [P, QT, E + 2])
        wsel = sb("wsel", [P, QT, E])
        wsum = sb("wsum", [P, QT])
        wsum1 = sb("wsum1", [P, QT])
        wrec = sb("wrec", [P, QT])
        wful = sb("wful", [P, QT, E])
        wsplit = sb("wsplit", [P, QT, 2 * E])
        w_ch = sb("w_ch", [P, TOK], F32R)
        raw = clip[:, 0:2].rearrange("p k c s -> p k (c s)")
        t_hi = k_st[:, 0:4].rearrange("p (k n) s -> p k (n s)", k=2)
        t_lo = k_st[:, 4:8].rearrange("p (k n) s -> p k (n s)", k=2)
        sel = k_st[:, 8].rearrange("p (k m) -> p k m", k=2)
        relu, sq, act = (scan[:, 2 * n:2 * n + 2].rearrange("p k c s -> p k (c s)") for n in range(3))
        act_hi, act_lo = (q_st[:, 4 * n:4 * n + 4].rearrange("p (k n) s -> p k (n s)", k=2) for n in range(2))
        res = f_sb[:].rearrange("p c (k s) -> p c k s", k=2)

        ld_in = [sem(f"ld_in{b}") for b in range(B)]
        ld_vec, ld_w, ld_gate = sem("ld_vec"), sem("ld_w"), sem("ld_gate")
        st_qk = sem("st_qk")
        ld_stack = [sem(f"ld_stack{h}") for h in range(KC)]
        ld_rows = [sem(f"ld_rows{h}") for h in range(KC)]
        ld_raw = [sem(f"ld_raw{i}") for i in range(2)]
        st_out = sem("st_out")
        pool_const, dve_const, ident_ready, tile_no_ready = sem("pool_const"), sem("dve_const"), sem("ident_ready"), sem("tile_no_ready")
        tsum_ready, setup_exp, setup_step, decay_ready = sem("tsum_ready"), sem("setup_exp"), sem("setup_step"), sem("decay_ready")
        clip_ready, ex_ready, pool_pre, pool_sum = sem("clip_ready"), sem("ex_ready"), sem("pool_pre"), sem("pool_sum")
        fwd_ready, bwd_ready, numden_ready, den_ready = sem("fwd_ready"), sem("bwd_ready"), sem("numden_ready"), sem("den_ready")
        ln1_ready, lnsum1_ready, rec1_ready, hid1_ready = sem("ln1_ready"), sem("lnsum1_ready"), sem("rec1_ready"), sem("hid1_ready")
        misc_full = [sem(f"misc_full{i}") for i in range(2)]
        misc_free = [sem(f"misc_free{i}") for i in range(2)]
        qk_hi_ready, qk_lo_ready, v_ready = sem("qk_hi_ready"), sem("qk_lo_ready"), sem("v_ready")
        s_ready, max_ready, nmax_hi_ready, nmax_lo_ready = sem("s_ready"), sem("max_ready"), sem("nmax_hi_ready"), sem("nmax_lo_ready")
        t_ready, prob_ready, pv_ready, o_raw_ready = sem("t_ready"), sem("prob_ready"), sem("pv_ready"), sem("o_raw_ready")
        rsum_ready, o_tok_ready, o_ch_ready, x1_ready = sem("rsum_ready"), sem("o_tok_ready"), sem("o_ch_ready"), sem("x1_ready")
        clip2_ready, ex2_ready, lne2_ready, lnsum2_ready, rec2_ready = sem("clip2_ready"), sem("ex2_ready"), sem("lne2_ready"), sem("lnsum2_ready"), sem("rec2_ready")
        hid2_ready, hid_hi_ready, hid_lo_ready = sem("hid2_ready"), sem("hid_hi_ready"), sem("hid_lo_ready")
        gex_ready, route, wsplit_ready, w_ch_ready = sem("gex_ready"), sem("route"), sem("wsplit_ready"), sem("w_ch_ready")
        up_hi_ready, up_lo_ready, dn_hi_ready, dn_lo_ready = sem("up_hi_ready"), sem("up_lo_ready"), sem("dn_hi_ready"), sem("dn_lo_ready")
        sel_ready, h_ready, wb_ready, relu_ready = sem("sel_ready"), sem("h_ready"), sem("wb_ready"), sem("relu_ready")
        sq_ready, act_ready, act_hi_ready, act_lo_ready = sem("sq_ready"), sem("act_ready"), sem("act_hi_ready"), sem("act_lo_ready")
        down_done, res_ready = sem("down_done"), sem("res_ready")

        def bank_s(n):
            return ps[:, n % 2, :].rearrange("p (t k) -> p t k", t=QT)

        def bank_t(n):
            return ps[:, 2 + n % 3, :].rearrange("p (t q) -> p t q", t=QT)

        bank_o = ps[:, 5, 0:S]
        jobs = []
        for b in range(B):
            if b == 0:
                jobs += [("q", 0), ("k", 0), ("v", 0)]
            jobs += [("m", b, 0)]
            if b > 0:
                jobs += [("gate", b - 1), ("wt", b - 1)]
            jobs += [("m", b, 1)]
            if b + 1 < B:
                jobs += [("q", b + 1), ("k", b + 1), ("v", b + 1)]
            jobs += [("ot", b, 0), ("ot", b, 1), ("oc", b), ("proj", b)]
        jobs += [("gate", B - 1), ("wt", B - 1)]
        job_no = {job: n for n, job in enumerate(jobs)}

        def job_bank(job):
            return ps[:, 6 + job_no[job] % 2, :]

        def job_begin(eng, job):
            n = job_no[job]
            if n >= 2:
                eng.wait_ge(misc_free[n % 2], n // 2)

        def job_sem(job):
            return misc_full[job_no[job] % 2]

        def job_wait(eng, job):
            n = job_no[job]
            eng.wait_ge(misc_full[n % 2], n // 2 + 1)

        def job_free(job):
            return misc_free[job_no[job] % 2]

        def bank_h(half):
            return ps[:, half, :]

        def bank_w(half):
            return ps[:, 6 + half, :]

        def bank_acc(oc, half):
            return ps[:, 2 + 2 * oc + half, :]

        def tok(b):
            return slice(b * S, (b + 1) * S)

        block = ctx.enter_context(nc.Block())

        @block.sync
        def _(sp):
            sp.dma_start(vec[:], vecs).then_inc(ld_vec, 16)
            sp.dma_start(cond_sb[:], cond.partition_broadcast(P)).then_inc(ld_vec, 16)
            for b in range(B):
                sp.dma_start(f_sb[:, :, tok(b)], fT[:, :, tok(b)]).then_inc(ld_in[b], 16)
                sp.dma_start(x_sb[:, :, tok(b)], xT[:, :, tok(b)]).then_inc(ld_in[b], 16)
                if b == 0:
                    sp.dma_start(wi[:], w_in).then_inc(ld_w, 16)
                    sp.dma_start(bvb[:], bv.partition_broadcast(P)).then_inc(ld_w, 16)
                    sp.dma_start(wo[:], w_out).then_inc(ld_w, 16)
            sp.dma_start(gw[:], gate_w).then_inc(ld_gate, 16)
            sp.dma_start(gbb[:], gate_bias.partition_broadcast(P)).then_inc(ld_gate, 16)

            def store_qk(b):
                sp.wait_ge(qk_hi_ready, 4 * (b + 1))
                sp.wait_ge(qk_lo_ready, 4 * (b + 1))
                for w in range(4):
                    part = (qk_hi, qk_lo)[w % 2]
                    sp.dma_start(qk_dram[w, :, tok(b)].rearrange("(t p) s -> p t s", p=P),
                                 part[:, w // 2, :, :].bitcast(F32)).then_inc(st_qk, 16)

            def load_stack(b, half):
                if b > 0:
                    sp.wait_ge(t_ready, H * (b - 1) + HB * (half + 1))
                for r in range(ROLE):
                    for st, w in ((q_st, r % 2), (k_st, 2 + r // 2)):
                        src = qk_dram[w, half * P:(half + 1) * P, tok(b)]
                        sp.dma_start(st[r * HD:(r + 1) * HD, half * HB:(half + 1) * HB, :].bitcast(F32),
                                     src.rearrange("(h d) s -> d h s", d=HD)).then_inc(ld_stack[half], 16)

            def load_rows(b, half):
                for n, (src, ready) in enumerate(((nmax_hi, nmax_hi_ready), (nmax_lo, nmax_lo_ready))):
                    sp.wait_ge(ready, KC * b + half + 1)
                    dst = q_st[MAXROW + n:MAXROW + n + 1, half * HB:(half + 1) * HB, :]
                    sp.dma_start(dst.rearrange("p h (t q) -> p (h t) q", t=QT).bitcast(F32),
                                 src[:, half, :].bitcast(F32)).then_inc(ld_rows[half], 16)

            store_qk(0)
            sp.wait_ge(st_qk, 64)
            for b in range(B):
                if b == 0:
                    load_stack(0, 0)
                    load_stack(0, 1)
                load_rows(b, 0)
                load_rows(b, 1)
                if b + 1 < B:
                    store_qk(b + 1)
                    sp.wait_ge(st_qk, 64 * (b + 2))
                    load_stack(b + 1, 0)
                    load_stack(b + 1, 1)

            sp.wait_ge(ex_ready, 4 * B)
            for i in range(2):
                sp.dma_start(raw[:, i, :], tiles[i]).then_inc(ld_raw[i], 16)
            with sp.Fori(0, NT // 2 - 1) as i:
                for k in range(2):
                    sp.wait_ge(dn_hi_ready, 2 * i + k + 1)
                    sp.wait_ge(dn_lo_ready, 2 * i + k + 1)
                    sp.dma_start(raw[:, k, :], tiles[2 * i + k + 2]).then_inc(ld_raw[k], 16)
            for oc in range(KC):
                for half in range(2):
                    sp.wait_ge(res_ready, 2 * oc + half + 1)
                    sp.dma_start(out[:, oc, half * HT:(half + 1) * HT], res[:, oc, half, :]).then_inc(st_out, 16)
            sp.wait_ge(st_out, 16 * 2 * KC)

        @block.gpsimd
        def _(pool):
            g = nc.gpsimd
            g.memset(ident[:], 0.0).then_inc(pool_const, 1)
            pool.wait_ge(pool_const, 1)
            g.affine_select(out=ident[:], in_=ident[:], compare_op=ALU.not_equal, fill=1.0, base=0,
                            pattern=[[-1, P]], channel_multiplier=1).then_inc(ident_ready, 1)
            g.iota(sel_i[:], pattern=[[-1, 2], [0, E]], base=0, channel_multiplier=1).then_inc(pool_const, 1)
            g.iota(tile_i[:], pattern=[[2, TILES]], base=0, channel_multiplier=0).then_inc(pool_const, 1)
            pool.wait_ge(pool_const, 3)
            g.tensor_copy(selval[:], sel_i[:]).then_inc(pool_const, 1)
            g.tensor_copy(tile_no[:], tile_i[:]).then_inc(tile_no_ready, 1)

            def recurrence(b):
                f = f_sb[:, :, tok(b)]
                pool.wait_ge(ld_in[b], 32)
                pool.wait_ge(ex_ready, 4 * b + 3)
                if b > 0:
                    pool.wait_ge(bwd_ready, 8 * b)
                g.tensor_tensor(ekv[:], ex[:, 0], f, ALU.mult).then_inc(pool_pre, 1)
                if b > 0:
                    pool.wait_ge(pool_sum, 4 * b)
                for n in range(2):
                    g.tensor_tensor(gk[:, n], ex[:, 1 + n], ex[:, 0], ALU.subtract).then_inc(pool_pre, 1)
                for n in range(2):
                    pool.wait_ge(pool_pre, 5 * b + 2 + n)
                    g.tensor_tensor(gkv[:, n], gk[:, n], f, ALU.mult).then_inc(pool_pre, 1)
                for n in range(2):
                    pool.wait_ge(fwd_ready, 8 * b + 2 * n + 2)
                    pool.wait_ge(pool_pre, 5 * b + 4 + n)
                    g.tensor_tensor(scan[:, n], scan[:, n], gkv[:, n], ALU.add).then_inc(pool_sum, 1)
                for n in range(2):
                    pool.wait_ge(fwd_ready, 8 * b + 4 + 2 * n + 2)
                    g.tensor_tensor(scan[:, 2 + n], scan[:, 2 + n], gk[:, n], ALU.add).then_inc(pool_sum, 1)

            def split_hidden(b):
                pool.wait_ge(hid_hi_ready, b + 1)
                g.tensor_tensor(hid_lo[:, :, tok(b)], hid2[:], hid_hi[:, :, tok(b)].bitcast(F32),
                                ALU.subtract).then_inc(hid_lo_ready, 1)

            recurrence(0)
            for b in range(B):
                if b > 0:
                    split_hidden(b - 1)
                if b + 1 < B:
                    recurrence(b + 1)
            split_hidden(B - 1)

            def square(n, half):
                pool.wait_ge(relu_ready, n + 1)
                g.tensor_tensor(sq[:, half], relu[:, half], relu[:, half], ALU.mult).then_inc(sq_ready, 1)

            for half in range(2):
                square(half, half)
            with pool.Fori(1, NT) as t:
                for half in range(2):
                    pool.wait_ge(act_hi_ready, 2 * t + half - 1)
                    pool.wait_ge(act_lo_ready, 2 * t + half - 1)
                    square(2 * t + half, half)

        @block.scalar
        def _(sc):
            a = nc.scalar
            sc.wait_ge(ld_vec, 32)
            for n, v in enumerate((V_W1, V_W2)):
                a.activation(dexp[:, n * KC:(n + 1) * KC], vec[:, v:v + KC], ACT.Exp).then_inc(setup_exp, 1)
            sc.wait_ge(setup_exp, 2)
            a.activation(dbase[:], dexp[:], ACT.Exp, scale=-1.0).then_inc(setup_exp, 1)
            sc.wait_ge(tsum_ready, 1)
            a.activation(tex[:], tsum[:], ACT.Exp, scale=-1.0).then_inc(setup_exp, 1)

            def exponentials(b):
                sc.wait_ge(clip_ready, 6 * (b + 1))
                if b > 0:
                    sc.wait_ge(pool_pre, 5 * b)
                    sc.wait_ge(bwd_ready, 8 * b)
                    sc.wait_ge(ln1_ready, 2 * b)
                for n in range(4):
                    a.activation(ex[:, n], clip[:, n], ACT.Exp, scale=1.0 if n < 3 else -1.0).then_inc(ex_ready, 1)
                sc.wait_ge(ex_ready, 4 * (b + 1))
                if b > 0:
                    sc.wait_ge(rec1_ready, b)
                a.activation(lne[:], ex[:, 3], ACT.Ln, bias=1.0).then_inc(ln1_ready, 1)

            def logs(b):
                if b > 0:
                    sc.wait_ge(rec1_ready, b)
                    sc.wait_ge(hid1_ready, b)
                sc.wait_ge(den_ready, 2 * b + 1)
                a.activation(lnd[:], den[:, b % 2, 0], ACT.Ln).then_inc(ln1_ready, 1)
                sc.wait_ge(lnsum1_ready, b + 1)
                a.activation(lne[:], lnd[:], ACT.Exp, scale=-1.0).then_inc(rec1_ready, 1)

            def evacuate_qk(b):
                sc.wait_ge(ld_vec, 32)
                if b > 0:
                    sc.wait_ge(st_qk, 64 * b)
                for w, v in enumerate((V_BQ, V_BK)):
                    job = ("qk"[w], b)
                    job_wait(sc, job)
                    for t in range(KC):
                        a.activation(qk_hi[:, w, t], job_bank(job)[:, t * S:(t + 1) * S], ACT.Identity,
                                     bias=vec[:, v + t:v + t + 1]).then_inc(qk_hi_ready, 1)

            def negate_max(b, half):
                job = ("m", b, half)
                job_wait(sc, job)
                if b > 0:
                    sc.wait_ge(ld_rows[half], 32 * b)
                a.activation(nmax_hi[:, half], job_bank(job)[0:H, 0:P], ACT.Copy, scale=-1.0).then_inc(nmax_hi_ready, 1)

            def probabilities(b, half):
                for h in range(half * HB, (half + 1) * HB):
                    n = H * b + h
                    sc.wait_ge(t_ready, n + 1)
                    if n >= PRING:
                        sc.wait_ge(pv_ready, (n - PRING) // 4 + 1)
                    a.activation(prob[:, n % PRING], bank_t(n), ACT.Exp, scale=SCALE).then_inc(prob_ready, 1)
                    if h % 4 == 3 and h > half * HB + 3:
                        evacuate_o(b, h // 4 - 1)
                evacuate_o(b, (half + 1) * HB // 4 - 1)

            def evacuate_o(b, grp):
                sc.wait_ge(pv_ready, 4 * b + grp + 1)
                if b > 0:
                    n = job_no[("ot", b - 1, 1)]
                    sc.wait_ge(misc_full[n % 2], n // 2 + 1)
                a.activation(o_raw[:, grp], bank_o, ACT.Copy).then_inc(o_raw_ready, 1)

            def evacuate_o_ch(b):
                job_wait(sc, ("oc", b))
                if b > 0:
                    n = job_no[("proj", b - 1)]
                    sc.wait_ge(misc_full[n % 2], n // 2 + 1)
                a.activation(o_ch[:], job_bank(("oc", b)).rearrange("p (t q) -> p t q", t=KC), ACT.Copy).then_inc(o_ch_ready, 1)
                sc.wait_ge(o_ch_ready, b + 1)
                sc.sem_inc(job_free(("oc", b)), 1)

            def second_exp(b):
                sc.wait_ge(clip2_ready, b + 1)
                if b > 0:
                    sc.wait_ge(lne2_ready, 2 * b)
                a.activation(ex2[:], clip2[:], ACT.Exp, scale=-1.0).then_inc(ex2_ready, 1)
                sc.wait_ge(ex2_ready, b + 1)
                if b > 0:
                    sc.wait_ge(hid2_ready, b)
                a.activation(lne2[:], ex2[:], ACT.Ln, bias=1.0).then_inc(lne2_ready, 1)
                sc.wait_ge(den_ready, 2 * b + 2)
                a.activation(lnd2[:], den[:, b % 2, 1], ACT.Ln).then_inc(lne2_ready, 1)

            def second_rec(b):
                sc.wait_ge(lnsum2_ready, b + 1)
                a.activation(lne2[:], lnd2[:], ACT.Exp, scale=-1.0).then_inc(rec2_ready, 1)
                sc.wait_ge(hid2_ready, b + 1)
                a.activation(hid_hi[:, :, tok(b)], hid2[:], ACT.Copy).then_inc(hid_hi_ready, 1)

            def gate_exp(b):
                job = ("gate", b)
                job_wait(sc, job)
                if b > 0:
                    sc.wait_ge(wsplit_ready, 2 * b)
                a.activation(gex[:], job_bank(job)[:, 0:QT * E].rearrange("p (t e) -> p t e", t=QT), ACT.Exp,
                             scale=-1.0).then_inc(gex_ready, 1)

            def evacuate_w(b):
                job_wait(sc, ("wt", b))
                a.activation(w_ch[:, tok(b)], job_bank(("wt", b))[:, 0:S], ACT.Copy).then_inc(w_ch_ready, 1)
                sc.wait_ge(w_ch_ready, b + 1)
                sc.sem_inc(job_free(("wt", b)), 1)

            exponentials(0)
            logs(0)
            evacuate_qk(0)
            for b in range(B):
                if b + 1 < B:
                    exponentials(b + 1)
                if b > 0:
                    second_exp(b - 1)
                    second_rec(b - 1)
                negate_max(b, 0)
                if b > 0:
                    gate_exp(b - 1)
                probabilities(b, 0)
                if b > 0:
                    evacuate_w(b - 1)
                negate_max(b, 1)
                if b + 1 < B:
                    logs(b + 1)
                    evacuate_qk(b + 1)
                probabilities(b, 1)
                evacuate_o_ch(b)
            second_exp(B - 1)
            second_rec(B - 1)
            gate_exp(B - 1)

            def split_up(k):
                sc.wait_ge(ld_raw[k], 16)
                a.activation(t_hi[:, k, 0:C], raw[:, k, 0:C], ACT.Copy).then_inc(up_hi_ready, 1)

            def split_down(k):
                a.activation(t_hi[:, k, C:2 * C], raw[:, k, C:2 * C], ACT.Copy).then_inc(dn_hi_ready, 1)

            def rectify(n, half):
                sc.wait_ge(h_ready, n + 1)
                a.activation(relu[:, half], bank_h(half), ACT.Relu).then_inc(relu_ready, 1)

            def round_act(n, half):
                sc.wait_ge(act_ready, n + 1)
                a.activation(act_hi[:, half], act[:, half], ACT.Copy).then_inc(act_hi_ready, 1)

            split_up(0)
            evacuate_w(B - 1)

            split_up(1)
            split_down(0)
            for half in range(2):
                rectify(half, half)
            for half in range(2):
                round_act(half, half)

            def tile(t, k, split=True, up_wait=None):
                if split:
                    sc.wait_ge(ld_raw[1 - k], up_wait)
                    sc.wait_ge(h_ready, 2 * t)
                    a.activation(t_hi[:, 1 - k, 0:C], raw[:, 1 - k, 0:C], ACT.Copy).then_inc(up_hi_ready, 1)
                if not isinstance(t, int) or t > 1:
                    sc.wait_ge(down_done, 2 * (t - 1))
                split_down(k)
                for half in range(2):
                    sc.wait_ge(sq_ready, 2 * (t - 1) + half + 1)
                    rectify(2 * t + half, half)
                for half in range(2):
                    sc.wait_ge(down_done, 2 * (t - 1) + half + 1)
                    round_act(2 * t + half, half)

            tile(1, 1, up_wait=32)
            with sc.Fori(1, NT // 2 - 1) as i:
                tile(2 * i, 0, up_wait=16 * i + 16)
                tile(2 * i + 1, 1, up_wait=16 * i + 32)
            tile(NT - 2, 0, up_wait=16 * (NT // 2))
            tile(NT - 1, 1, split=False)

        @block.vector
        def _(dve):
            v = nc.vector
            TT = v.tensor_tensor
            v.memset(v_aug[:], 1.0).then_inc(dve_const, 1)
            v.memset(q_st[STACK:P].bitcast(F32), 0.0).then_inc(dve_const, 1)
            v.memset(k_st[STACK:MAXROW].bitcast(F32), 0.0).then_inc(dve_const, 1)
            v.memset(k_st[MAXROW:P].bitcast(F32), 1.0).then_inc(dve_const, 1)
            v.memset(gsum[:, :, G:G + 4], NONE).then_inc(dve_const, 1)
            v.memset(masked[:, :, E:E + 2], NONE).then_inc(dve_const, 1)
            dve.wait_ge(pool_const, 4)
            v.tensor_scalar(selval[E:P, :], selval[E:P, :], float(-E), None, ALU.add).then_inc(dve_const, 1)

            def clips(b):
                if b == 0:
                    dve.wait_ge(ld_vec, 32)
                dve.wait_ge(ld_in[b], 32)
                if b > 0:
                    dve.wait_ge(ex_ready, 4 * b)
                f = f_sb[:, :, tok(b)]
                v.tensor_scalar(clip[:, 0], f, 30.0, None, ALU.min).then_inc(clip_ready, 1)
                for n, u in enumerate((V_U1, V_U2)):
                    for c in range(KC):
                        v.tensor_scalar(clip[:, 1 + n, c], f[:, c], vec[:, u + c:u + c + 1], 30.0,
                                        ALU.add, ALU.min).then_inc(clip_ready, 1)
                v.tensor_scalar(clip[:, 3], x_sb[:, :, tok(b)], -41.0, None, ALU.max).then_inc(clip_ready, 1)

            clips(0)
            v.tensor_reduce(tsum[:], cond_sb[:], AX_X, ALU.add).then_inc(tsum_ready, 1)
            dve.wait_ge(setup_exp, 4)
            v.tensor_scalar(tden[:], tex[:], 1.0, None, ALU.add).then_inc(setup_step, 1)
            dve.wait_ge(setup_step, 1)
            v.reciprocal(tf[:], tden[:]).then_inc(setup_step, 1)
            dve.wait_ge(setup_step, 2)
            v.tensor_scalar(thalf[:], tf[:], 0.5, 0.5, ALU.mult, ALU.add).then_inc(setup_step, 1)
            v.tensor_scalar(cfac[:], tf[:], 0.2, 0.8, ALU.mult, ALU.add).then_inc(setup_step, 1)
            dve.wait_ge(setup_step, 4)
            for n in range(2 * KC):
                v.tensor_scalar(decay[:, n], thalf[:], dbase[:, n:n + 1], None, ALU.mult).then_inc(decay_ready, 1)

            def scans(b):
                if b == 0:
                    dve.wait_ge(decay_ready, 2 * KC)
                for back in range(2):
                    for which in range(2):
                        if back == 0:
                            dve.wait_ge(pool_pre, 5 * b + 1) if which == 0 else dve.wait_ge(ex_ready, 4 * b + 1)
                            if b > 0:
                                dve.wait_ge(numden_ready, 4 * b)
                        for n in range(2):
                            for c in range(KC):
                                src = (ekv[:, c], ex[:, 0, c])[which]
                                dst = scan[:, 4 * back + 2 * which + n, c]
                                if back:
                                    src, dst = src[:, ::-1], dst[:, ::-1]
                                v.tensor_tensor_scan(dst, decay[:, n * KC + c, b:b + 1].broadcast_to([P, S]), src, 0.0,
                                                     ALU.mult, ALU.add).then_inc((fwd_ready, bwd_ready)[back], 1)

            def num_den(b):
                if b > 1:
                    dve.wait_ge(hid2_ready, b - 1)
                for which in range(2):
                    for n in range(2):
                        dve.wait_ge(pool_sum, 4 * b + 2 * which + n + 1)
                        dve.wait_ge(bwd_ready, 8 * b + 4 * which + 2 * n + 2)
                        row = 2 * which + n
                        dst = (num, den)[which][:, b % 2, n]
                        TT(dst, scan[:, row], scan[:, 4 + row], ALU.add).then_inc(numden_ready, 1)
                for n in range(2):
                    dve.wait_ge(numden_ready, 4 * b + 3 + n)
                    d = den[:, b % 2, n]
                    v.tensor_scalar(d, d, 1e-8, None, ALU.max).then_inc(den_ready, 1)

            def hidden1(b):
                dve.wait_ge(ln1_ready, 2 * (b + 1))
                TT(lnd[:], lnd[:], lne[:], ALU.add).then_inc(lnsum1_ready, 1)
                dve.wait_ge(rec1_ready, b + 1)
                if b > 0:
                    dve.wait_ge(v_ready, QT * b)
                v.scalar_tensor_tensor(hid1[:], num[:, b % 2, 0], cfac[:, b:b + 1], lne[:], ALU.mult,
                                       ALU.mult).then_inc(hid1_ready, 1)

            def split_qk(b):
                for w, u in enumerate((V_BQ, V_BK)):
                    job = ("qk"[w], b)
                    dve.wait_ge(qk_hi_ready, 4 * b + 2 * w + 2)
                    for t in range(KC):
                        last = v.scalar_tensor_tensor(qk_lo[:, w, t], job_bank(job)[:, t * S:(t + 1) * S],
                                                      vec[:, u + t:u + t + 1], qk_hi[:, w, t].bitcast(F32), ALU.add,
                                                      ALU.subtract).then_inc(qk_lo_ready, 1)
                    dve.wait_ge(qk_lo_ready, 4 * b + 2 * w + 2)
                    dve.sem_inc(job_free(job), 1)

            def add_v_bias(b):
                job = ("v", b)
                job_wait(dve, job)
                for t in range(QT):
                    if b > 1 and t == 0:
                        dve.wait_ge(pv_ready, 4 * (b - 1))
                    src = job_bank(job)[:, t * C:(t + 1) * C].rearrange("p (h d) -> p h d", d=HD)
                    TT(v_aug[:, b % 2, t, :, 0:HD], src, bvb[:].rearrange("p (h d) -> p h d", d=HD),
                       ALU.add).then_inc(v_ready, 1)
                dve.wait_ge(v_ready, QT * (b + 1))
                dve.sem_inc(job_free(job), 1)

            def maximum(b, h):
                n = H * b + h
                dve.wait_ge(s_ready, n + 1)
                if b > 1 and h == 0:
                    n2 = job_no[("m", b - 2, 1)]
                    dve.wait_ge(misc_full[n2 % 2], n2 // 2 + 1)
                v.tensor_reduce(mx[:, b % 2, h], bank_s(n), AX_X, ALU.max).then_inc(max_ready, 1)

            def low_max(b, half):
                job = ("m", b, half)
                dve.wait_ge(nmax_hi_ready, KC * b + half + 1)
                v.scalar_tensor_tensor(nmax_lo[:, half], job_bank(job)[0:H, 0:P], -1.0, nmax_hi[:, half].bitcast(F32),
                                       ALU.mult, ALU.subtract).then_inc(nmax_lo_ready, 1)
                dve.wait_ge(nmax_lo_ready, KC * b + half + 1)
                dve.sem_inc(job_free(job), 1)

            def normalise(b):
                for qt in range(QT):
                    job = ("ot", b, qt)
                    job_wait(dve, job)
                    src = job_bank(job).rearrange("p (h c) -> p h c", c=32)
                    if b > 0 and qt == 0:
                        n = job_no[("oc", b - 1)]
                        dve.wait_ge(misc_full[n % 2], n // 2 + 1)
                    v.reciprocal(rsum[:, qt], src[:, :, HD]).then_inc(rsum_ready, 1)
                    dve.wait_ge(rsum_ready, QT * b + qt + 1)
                    TT(o_tok[:, qt], src[:, :, 0:HD], rsum[:, qt].unsqueeze(2).broadcast_to([P, H, HD]),
                       ALU.mult).then_inc(o_tok_ready, 1)
                    dve.wait_ge(o_tok_ready, QT * b + qt + 1)
                    dve.sem_inc(job_free(job), 1)

            def residual(b):
                job = ("proj", b)
                job_wait(dve, job)
                for c in range(KC):
                    v.scalar_tensor_tensor(x1[:, c, tok(b)], job_bank(job)[:, c * S:(c + 1) * S],
                                           vec[:, V_BP + c:V_BP + c + 1], x_sb[:, c, tok(b)], ALU.add,
                                           ALU.add).then_inc(x1_ready, 1)
                dve.wait_ge(x1_ready, KC * (b + 1))
                dve.sem_inc(job_free(job), 1)
                if b > 0:
                    dve.wait_ge(ex2_ready, b)
                v.tensor_scalar(clip2[:], x1[:, :, tok(b)], -41.0, None, ALU.max).then_inc(clip2_ready, 1)

            def lnsum2(b):
                dve.wait_ge(lne2_ready, 2 * (b + 1))
                TT(lnd2[:], lnd2[:], lne2[:], ALU.add).then_inc(lnsum2_ready, 1)

            def hidden2(b):
                dve.wait_ge(rec2_ready, b + 1)
                if b > 0:
                    dve.wait_ge(hid_hi_ready, b)
                    dve.wait_ge(hid_lo_ready, b)
                    n = job_no[("gate", b - 1)]
                    dve.wait_ge(misc_full[n % 2], n // 2 + 1)
                v.scalar_tensor_tensor(hid2[:], num[:, b % 2, 1], cfac[:, b:b + 1], lne2[:], ALU.mult,
                                       ALU.mult).then_inc(hid2_ready, 1)

            def router(b):
                count = [b * ROUTE_STEPS]

                def step(ins):
                    ins.then_inc(route, 1)
                    count[0] += 1
                    dve.wait_ge(route, count[0])

                if b == 0:
                    dve.wait_ge(ld_gate, 32)
                dve.wait_ge(gex_ready, b + 1)
                dve.sem_inc(job_free(("gate", b)), 1)
                step(v.tensor_scalar(gden[:], gex[:], 1.0, None, ALU.add))
                step(v.reciprocal(score[:], gden[:]))
                for t in range(QT):
                    step(TT(sbias[:, t], score[:, t].rearrange("p (g e) -> p g e", g=G),
                            gbb[:].rearrange("p (g e) -> p g e", g=G), ALU.add))
                pairs = sbias[:].rearrange("p t g (a c) -> p (t g) a c", c=2)
                step(TT(pmax[:], pairs[:, :, :, 0], pairs[:, :, :, 1], ALU.max))
                step(TT(pmin[:], pairs[:, :, :, 0], pairs[:, :, :, 1], ALU.min))
                for best, low, nbest, mid, nlow, nsec, w in ((pmax, pmin, qmax, qmid, qlow, qsec, 2),
                                                             (qmax, qsec, fmax, fmid, flow, fsec, 1)):
                    step(TT(nbest[:], best[:, :, 0:w], best[:, :, w:2 * w], ALU.max))
                    step(TT(mid[:], best[:, :, 0:w], best[:, :, w:2 * w], ALU.min))
                    step(TT(nlow[:], low[:, :, 0:w], low[:, :, w:2 * w], ALU.max))
                    step(TT(nsec[:], mid[:], nlow[:], ALU.max))
                step(TT(gsum[:, :, 0:G], fmax[:, :, 0].rearrange("p (t g) -> p t g", t=QT),
                        fsec[:, :, 0].rearrange("p (t g) -> p t g", t=QT), ALU.add))
                for t in range(QT):
                    step(v.max(gtop[:, t], gsum[:, t, 0:G]))
                step(v.memset(gtop[:, :, GT:8], NONE))
                for t in range(QT):
                    step(v.match_replace(grep[:, t], gtop[:, t], gsum[:, t], BIG))
                step(v.tensor_scalar(gpen[:], grep[:, :, 0:G], BIG, -BIG, ALU.is_lt, ALU.mult))
                for t in range(QT):
                    step(TT(masked[:, t, 0:E].rearrange("p (g e) -> p g e", g=G), sbias[:, t],
                            gpen[:, t].unsqueeze(2).broadcast_to([P, G, EG]), ALU.add))
                for t in range(QT):
                    step(v.max(etop[:, t], masked[:, t, 0:E]))
                step(v.memset(etop[:, :, TOPK:8], NONE))
                for t in range(QT):
                    step(v.match_replace(erep[:, t], etop[:, t], masked[:, t], BIG))
                step(v.scalar_tensor_tensor(wsel[:], erep[:, :, 0:E], BIG, score[:], ALU.is_ge, ALU.mult))
                step(v.tensor_reduce(wsum[:], wsel[:], AX_X, ALU.add))
                step(v.tensor_scalar(wsum1[:], wsum[:], 1e-20, None, ALU.add))
                step(v.reciprocal(wrec[:], wsum1[:]))
                for t in range(QT):
                    step(v.tensor_scalar(wful[:, t], wsel[:, t], wrec[:, t:t + 1], 2.5, ALU.mult, ALU.mult))
                assert count[0] == (b + 1) * ROUTE_STEPS, count[0]
                if b > 0:
                    n = job_no[("wt", b - 1)]
                    dve.wait_ge(misc_full[n % 2], n // 2 + 1)
                v.tensor_copy(wsplit[:, :, 0:E].bitcast(F32R), wful[:]).then_inc(wsplit_ready, 1)
                dve.wait_ge(wsplit_ready, 2 * b + 1)
                TT(wsplit[:, :, E:2 * E].bitcast(F32R), wful[:], wsplit[:, :, 0:E], ALU.subtract).then_inc(wsplit_ready, 1)

            ROUTE_STEPS = 34

            scans(0)
            num_den(0)
            hidden1(0)
            dve.wait_ge(ld_w, 48)
            split_qk(0)
            add_v_bias(0)
            for b in range(B):
                if b + 1 < B:
                    clips(b + 1)
                for h in range(HB):
                    maximum(b, h)
                    if b > 0 and h == 1:
                        lnsum2(b - 1)
                    if b > 0 and h == 3:
                        hidden2(b - 1)
                low_max(b, 0)
                for h in range(HB, H):
                    maximum(b, h)
                    if b > 0 and h == HB:
                        router(b - 1)
                low_max(b, 1)
                if b + 1 < B:
                    scans(b + 1)
                    num_den(b + 1)
                    hidden1(b + 1)
                    split_qk(b + 1)
                    add_v_bias(b + 1)
                normalise(b)
                residual(b)
            lnsum2(B - 1)
            hidden2(B - 1)
            router(B - 1)

            def split_up(k):
                TT(t_lo[:, k, 0:C], raw[:, k, 0:C], t_hi[:, k, 0:C].bitcast(F32), ALU.subtract).then_inc(up_lo_ready, 1)

            def split_down(k):
                TT(t_lo[:, k, C:2 * C], raw[:, k, C:2 * C], t_hi[:, k, C:2 * C].bitcast(F32),
                   ALU.subtract).then_inc(dn_lo_ready, 1)

            def select(t, k):
                v.tensor_scalar(sel[:, k], selval[:], tile_no[:, bass.ds(t, 1)], None, ALU.is_equal).then_inc(sel_ready, 1)

            def gated(n, half):
                dve.wait_ge(sq_ready, n + 1)
                dve.wait_ge(wb_ready, n + 1)
                TT(act[:, half], sq[:, half], bank_w(half), ALU.mult).then_inc(act_ready, 1)

            def shared(n, half):
                dve.wait_ge(sq_ready, n + 1)
                v.tensor_copy(act[:, half], sq[:, half]).then_inc(act_ready, 1)

            def low_act(n, half):
                dve.wait_ge(act_hi_ready, n + 1)
                TT(act_lo[:, half], act[:, half], act_hi[:, half].bitcast(F32), ALU.subtract).then_inc(act_lo_ready, 1)

            dve.wait_ge(tile_no_ready, 1)
            dve.wait_ge(dve_const, 7)
            dve.wait_ge(up_hi_ready, 1)
            split_up(0)
            select(0, 0)
            dve.wait_ge(up_hi_ready, 2)
            split_up(1)
            select(1, 1)
            dve.wait_ge(dn_hi_ready, 1)
            split_down(0)
            for half in range(2):
                gated(half, half)
                low_act(half, half)

            def tile(t, k, mult=gated, split=True, pick=True):
                if split:
                    dve.wait_ge(up_hi_ready, t + 2)
                    split_up(1 - k)
                if pick:
                    dve.wait_ge(wb_ready, 2 * t)
                    select(t + 1, 1 - k)
                dve.wait_ge(dn_hi_ready, t + 1)
                split_down(k)
                for half in range(2):
                    mult(2 * t + half, half)
                    dve.wait_ge(down_done, 2 * (t - 1) + half + 1)
                    low_act(2 * t + half, half)

            tile(1, 1)
            with dve.Fori(1, TILES // 2 - 1) as i:
                tile(2 * i, 0)
                tile(2 * i + 1, 1)
            tile(TILES - 2, 0)
            tile(TILES - 1, 1, pick=False)
            tile(TILES, 0, mult=shared, pick=False)
            tile(TILES + 1, 1, mult=shared, split=False, pick=False)
            dve.wait_ge(down_done, 2 * NT)
            for oc in range(KC):
                for half in range(2):
                    TT(res[:, oc, half], bank_acc(oc, half), x1[:, oc, half * HT:(half + 1) * HT],
                       ALU.add).then_inc(res_ready, 1)

        @block.tensor
        def _(pe):
            mm = nc.tensor.matmul

            def project(b):
                pe.wait_ge(hid1_ready, b + 1)
                for w, name in enumerate("qk"):
                    job = (name, b)
                    job_begin(pe, job)
                    for t in range(KC):
                        for c in range(KC):
                            last = mm(job_bank(job)[:, t * S:(t + 1) * S], wi[:, c, w * C + t * P:w * C + (t + 1) * P],
                                      hid1[:, c, :], start=(c == 0), stop=(c == KC - 1))
                    last.then_inc(job_sem(job), 1)
                job = ("v", b)
                job_begin(pe, job)
                for t in range(QT):
                    for c in range(KC):
                        last = mm(job_bank(job)[:, t * C:(t + 1) * C], hid1[:, c, t * P:(t + 1) * P],
                                  wi[:, c, 2 * C:3 * C], start=(c == 0), stop=(c == KC - 1))
                last.then_inc(job_sem(job), 1)

            def scores(b, h):
                n = H * b + h
                if h % HB == 0:
                    pe.wait_ge(ld_stack[h // HB], 16 * 2 * ROLE * (b + 1))
                if n >= 2:
                    pe.wait_ge(max_ready, n - 1)
                for qt in range(QT):
                    last = mm(bank_s(n)[:, qt], q_st[0:MAXROW, h, qt * P:(qt + 1) * P], k_st[0:MAXROW, h, :],
                              start=True, stop=True)
                last.then_inc(s_ready, 1)

            def turn_max(b, half):
                job = ("m", b, half)
                job_begin(pe, job)
                pe.wait_ge(max_ready, H * b + HB * (half + 1))
                nc.tensor.transpose(job_bank(job)[0:H, 0:P],
                                    mx[:, b % 2, half * HB:(half + 1) * HB].rearrange("p h t -> p (h t)"),
                                    ident[:]).then_inc(job_sem(job), 1)

            def shifted_scores(b, h):
                n = H * b + h
                if h % HB == 0:
                    pe.wait_ge(ld_rows[h // HB], 32 * (b + 1))
                if n >= 3:
                    pe.wait_ge(prob_ready, n - 2)
                for kt in range(QT):
                    last = mm(bank_t(n)[:, kt], k_st[0:MAXROW + 2, h, kt * P:(kt + 1) * P], q_st[0:MAXROW + 2, h, :],
                              start=True, stop=True)
                last.then_inc(t_ready, 1)

            def values(b, grp):
                if 4 * b + grp > 0:
                    pe.wait_ge(o_raw_ready, 4 * b + grp)
                pe.wait_ge(v_ready, QT * (b + 1))
                pe.wait_ge(prob_ready, H * b + 4 * grp + 4)
                for kt in range(QT):
                    for j in range(4):
                        h = 4 * grp + j
                        last = mm(bank_o[32 * j:32 * j + 32, :], v_aug[:, b % 2, kt, h, :],
                                  prob[:, (H * b + h) % PRING, kt, :], start=(kt == 0), stop=(kt == QT - 1))
                last.then_inc(pv_ready, 1)

            def turn_out(b):
                pe.wait_ge(o_raw_ready, 4 * (b + 1))
                for qt in range(QT):
                    job = ("ot", b, qt)
                    job_begin(pe, job)
                    for grp in range(4):
                        last = nc.tensor.transpose(job_bank(job)[:, grp * P:(grp + 1) * P],
                                                   o_raw[:, grp, qt * P:(qt + 1) * P], ident[:])
                    last.then_inc(job_sem(job), 1)
                job = ("oc", b)
                job_begin(pe, job)
                pe.wait_ge(o_tok_ready, QT * (b + 1))
                for c in range(KC):
                    for qt in range(QT):
                        last = nc.tensor.transpose(job_bank(job)[:, c * S + qt * P:c * S + (qt + 1) * P],
                                                   o_tok[:, qt, c * HB:(c + 1) * HB].rearrange("p h d -> p (h d)"), ident[:])
                last.then_inc(job_sem(job), 1)
                job = ("proj", b)
                job_begin(pe, job)
                pe.wait_ge(o_ch_ready, b + 1)
                for t in range(KC):
                    for c in range(KC):
                        last = mm(job_bank(job)[:, t * S:(t + 1) * S], wo[:, c, t * P:(t + 1) * P], o_ch[:, c, :],
                                  start=(c == 0), stop=(c == KC - 1))
                last.then_inc(job_sem(job), 1)

            def gate(b):
                job = ("gate", b)
                job_begin(pe, job)
                pe.wait_ge(ld_gate, 32)
                pe.wait_ge(hid2_ready, b + 1)
                for t in range(QT):
                    for c in range(KC):
                        last = mm(job_bank(job)[:, t * E:(t + 1) * E], hid2[:, c, t * P:(t + 1) * P], gw[:, c, :],
                                  start=(c == 0), stop=(c == KC - 1))
                last.then_inc(job_sem(job), 1)

            def turn_weights(b):
                job = ("wt", b)
                job_begin(pe, job)
                pe.wait_ge(wsplit_ready, 2 * (b + 1))
                for t in range(QT):
                    last = nc.tensor.transpose(job_bank(job)[:, t * P:(t + 1) * P], wsplit[:, t], ident[:])
                last.then_inc(job_sem(job), 1)

            pe.wait_ge(ld_w, 48)
            project(0)
            pe.wait_ge(ident_ready, 1)
            pe.wait_ge(dve_const, 6)
            for b in range(B):
                for h in range(HB):
                    scores(b, h)
                turn_max(b, 0)
                if b > 0:
                    gate(b - 1)
                scores(b, HB)
                scores(b, HB + 1)
                if b > 0:
                    turn_weights(b - 1)
                for h in range(HB + 2, H):
                    scores(b, h)
                for h in range(HB):
                    shifted_scores(b, h)
                    if h == 5:
                        values(b, 0)
                values(b, 1)
                turn_max(b, 1)
                if b + 1 < B:
                    project(b + 1)
                for h in range(HB, H):
                    shifted_scores(b, h)
                    if h == HB + 5:
                        values(b, 2)
                values(b, 3)
                turn_out(b)
            gate(B - 1)
            turn_weights(B - 1)

            def up(t, k, half, wb=True):
                for c in range(KC):
                    w_hi, w_lo = (w[:, k, c * P:(c + 1) * P] for w in (t_hi, t_lo))
                    x_hi, x_lo = (x[:, c, half * HT:(half + 1) * HT] for x in (hid_hi, hid_lo))
                    mm(bank_h(half), w_hi, x_hi, start=(c == 0), stop=False)
                    mm(bank_h(half), w_hi, x_lo, start=False, stop=False)
                    last = mm(bank_h(half), w_lo, x_hi, start=False, stop=(c == KC - 1))
                last.then_inc(h_ready, 1)
                if wb:
                    mm(bank_w(half), sel[:, k], w_ch[:, half * HT:(half + 1) * HT], start=True,
                       stop=True).then_inc(wb_ready, 1)

            def down(k, half, first=False, final=False):
                for oc in range(KC):
                    w_hi, w_lo = (w[:, k, C + oc * P:C + (oc + 1) * P] for w in (t_hi, t_lo))
                    acc = bank_acc(oc, half)
                    mm(acc, w_hi, act_hi[:, half], start=first, stop=False, skip_group_check=True)
                    mm(acc, w_hi, act_lo[:, half], start=False, stop=False, skip_group_check=True)
                    last = mm(acc, w_lo, act_hi[:, half], start=False, stop=final, skip_group_check=True)
                last.then_inc(down_done, 1)

            def step(t, k, wb=True, first=False):
                pe.wait_ge(up_lo_ready, t + 1)
                if wb:
                    pe.wait_ge(sel_ready, t + 1)
                for half in range(2):
                    pe.wait_ge(relu_ready, 2 * (t - 1) + half + 1)
                    if wb:
                        pe.wait_ge(act_ready, 2 * (t - 1) + half + 1)
                    up(t, k, half, wb)
                pe.wait_ge(dn_lo_ready, t)
                for half in range(2):
                    pe.wait_ge(act_lo_ready, 2 * (t - 1) + half + 1)
                    down(1 - k, half, first)

            pe.wait_ge(hid_lo_ready, B)
            pe.wait_ge(hid_hi_ready, B)
            pe.wait_ge(w_ch_ready, B)
            pe.wait_ge(up_lo_ready, 1)
            pe.wait_ge(sel_ready, 1)
            for half in range(2):
                up(0, 0, half)
            step(1, 1, first=True)
            with pe.Fori(1, TILES // 2) as i:
                step(2 * i, 0)
                step(2 * i + 1, 1)
            step(TILES, 0, wb=False)
            step(TILES + 1, 1, wb=False)
            pe.wait_ge(dn_lo_ready, NT)
            for half in range(2):
                pe.wait_ge(act_lo_ready, 2 * (NT - 1) + half + 1)
                down(1, half, final=True)


def kernel(**inputs):
    import numpy as np
    import concourse.bacc as bacc
    from concourse.bass_utils import run_bass_kernel_spmd

    def arr(name):
        return np.asarray(inputs[name])

    def chunks(a):
        return np.ascontiguousarray(a.reshape(KC, P, -1).transpose(1, 0, 2))

    x, f = arr("x"), arr("fside_BxSxS_0")
    wqkv = arr("L0_attn_Wqkv").reshape(H, 3, HD, C).transpose(1, 0, 2, 3).reshape(3 * C, C)
    bqkv = arr("L0_attn_bqkv").reshape(H, 3, HD).transpose(1, 0, 2).reshape(3, C)
    cols = [arr("L0_cond_w"), arr("L0_cond_u"), arr("L0_cond2_w"), arr("L0_cond2_u"), bqkv[0], bqkv[1],
            arr("L0_attn_bproj")]
    up = np.concatenate([arr("L0_ffn_w1").reshape(E * I, C), arr("L0_ffn_shared_up")])
    down = np.concatenate([arr("L0_ffn_w2").transpose(0, 2, 1).reshape(E * I, C), arr("L0_ffn_shared_down").T])
    up = up.reshape(NT, P, KC, P).transpose(0, 3, 2, 1).reshape(NT, P, C)
    arrays = {
        "xT": chunks(x.reshape(TOK, C).T),
        "fT": chunks(f.reshape(TOK, C).T),
        "cond": arr("cond_512"),
        "vecs": np.concatenate([v.reshape(KC, P).T for v in cols], axis=1),
        "w_in": chunks(wqkv.T),
        "w_out": chunks(arr("L0_attn_Wproj").T),
        "gate_w": chunks(arr("L0_ffn_gate_w").T),
        "bv": bqkv[2],
        "gate_bias": arr("L0_ffn_gate_bias"),
        "tiles": np.concatenate([up, down.reshape(NT, P, C)], axis=2),
    }
    arrays = {f"in_{n}": np.ascontiguousarray(a) for n, a in arrays.items()}
    nc = bacc.Bacc("TRN2", target_bir_lowering=False, num_devices=1)
    args = [nc.dram_tensor(n, a.shape, mybir.dt.from_np(a.dtype), kind="ExternalInput").ap() for n, a in arrays.items()]
    out = nc.dram_tensor("out", (P, KC, TOK), F32, kind="ExternalOutput").ap()
    bass_adaln_attn_ffn(nc, *args, out)
    r = run_bass_kernel_spmd(nc, [arrays], core_ids=[0])
    y = r.results[0]["out"]
    return np.ascontiguousarray(y.transpose(2, 1, 0).reshape(B, S, C))
```

```python
from contextlib import ExitStack

import concourse.bass as bass
from concourse import mybir

P = 128
B, S, C = 4, 256, 256
TOK = B * S
KC = C // P
H, HD = 16, 16
HB = H // KC
QT = S // P
E, I = 64, 64
G, GT, TOPK = 8, 4, 6
EG = E // G
TILES = E * I // P
SHARED = 256 // P
NT = TILES + SHARED
TD = 64
ROLE = 4
STACK = ROLE * HD
MAXROW = 96
HT = 512
SCALE = float(HD) ** 0.5
SLOTS = 3
PRING = 6
BIG = 1.0e30
NONE = -3.0e38

F32 = mybir.dt.float32
F32R = mybir.dt.float32r
I32 = mybir.dt.int32
ALU = mybir.AluOpType
ACT = mybir.ActivationFunctionType
AX_X = mybir.AxisListType.X

V_W1, V_U1, V_W2, V_U2, V_BQ, V_BK, V_BP = (KC * n for n in range(7))
NVEC = 7 * KC


def bass_adaln_attn_ffn(nc, xT, fT, cond, vecs, w_in, w_out, gate_w, bv, gate_bias, tiles, out):
    qk_dram = nc.dram_tensor("qk_split", (4, C, TOK), F32, kind="Internal").ap()

    with ExitStack() as ctx:
        def sb(name, shape, dt=F32):
            return ctx.enter_context(nc.sbuf_tensor(name, shape, dt))

        def sem(name):
            return ctx.enter_context(nc.semaphore(name))

        ps = ctx.enter_context(nc.psum_tensor("ps", [P, 8, 512], F32))

        x_sb = sb("x_sb", [P, KC, TOK])
        f_sb = sb("f_sb", [P, KC, TOK])
        vec = sb("vec", [P, NVEC])
        cond_sb = sb("cond_sb", [P, B, TD])
        wi = sb("wi", [P, KC, 3 * C])
        wo = sb("wo", [P, KC, C])
        gw = sb("gw", [P, KC, E])
        bvb = sb("bvb", [P, C])
        gbb = sb("gbb", [P, E])
        ident = sb("ident", [P, P])
        selval = sb("selval", [P, P])
        sel_i = sb("sel_i", [P, P], I32)
        tile_i = sb("tile_i", [P, TILES], I32)
        tile_no = sb("tile_no", [P, TILES])
        tsum = sb("tsum", [P, B])
        tex = sb("tex", [P, B])
        tden = sb("tden", [P, B])
        tf = sb("tf", [P, B])
        thalf = sb("thalf", [P, B])
        cfac = sb("cfac", [P, B])
        dexp = sb("dexp", [P, 2 * KC])
        dbase = sb("dbase", [P, 2 * KC])
        decay = sb("decay", [P, 2 * KC, B])
        clip = sb("clip", [P, 4, KC, S])
        gkv = clip[:, 0:2]
        ex = sb("ex", [P, 4, KC, S])
        gk = ex[:, 1:3]
        ekv = sb("ekv", [P, KC, S])
        scan = sb("scan", [P, 8, KC, S])
        num1 = sb("num1", [P, KC, S])
        den1 = sb("den1", [P, KC, S])
        num2 = sb("num2", [P, 2, KC, S])
        den2 = sb("den2", [P, 2, KC, S])
        hid1 = sb("hid1", [P, KC, S])
        qk_hi = sb("qk_hi", [P, 2, KC, S], F32R)
        qk_lo = sb("qk_lo", [P, 2, KC, S], F32R)
        v_aug = sb("v_aug", [P, 2, QT, H, 32])
        fill = sb("fill", [P, S])
        q_st = sb("q_st", [P, SLOTS, HB, S], F32R)
        k_st = sb("k_st", [P, SLOTS, HB, S], F32R)
        mx = sb("mx", [P, 2, H, QT])
        nmax_hi = sb("nmax_hi", [H, KC, P], F32R)
        nmax_lo = sb("nmax_lo", [H, KC, P], F32R)
        prob = sb("prob", [P, PRING, QT, S])
        o_raw = sb("o_raw", [P, 4, S])
        rsum = sb("rsum", [P, QT, H])
        o_tok = sb("o_tok", [P, QT, H, HD])
        o_ch = sb("o_ch", [P, KC, S])
        x1 = sb("x1", [P, KC, TOK])
        ex2 = sb("ex2", [P, KC, S])
        hid2 = sb("hid2", [P, KC, S])
        hid_hi = sb("hid_hi", [P, KC, TOK], F32R)
        hid_lo = sb("hid_lo", [P, KC, TOK], F32R)
        gex = sb("gex", [P, QT, E])
        gden = sb("gden", [P, QT, E])
        score = sb("score", [P, QT, E])
        sbias = sb("sbias", [P, QT, G, EG])
        pmax = sb("pmax", [P, QT * G, 4])
        pmin = sb("pmin", [P, QT * G, 4])
        qmax = sb("qmax", [P, QT * G, 2])
        qmid = sb("qmid", [P, QT * G, 2])
        qlow = sb("qlow", [P, QT * G, 2])
        qsec = sb("qsec", [P, QT * G, 2])
        fmax = sb("fmax", [P, QT * G, 1])
        fmid = sb("fmid", [P, QT * G, 1])
        flow = sb("flow", [P, QT * G, 1])
        fsec = sb("fsec", [P, QT * G, 1])
        gsum = sb("gsum", [P, QT, G + 4])
        gtop = sb("gtop", [P, QT, 8])
        grep = sb("grep", [P, QT, G + 4])
        gpen = sb("gpen", [P, QT, G])
        masked = sb("masked", [P, QT, E + 2])
        etop = sb("etop", [P, QT, 8])
        erep = sb("erep", [P, QT, E + 2])
        wsel = sb("wsel", [P, QT, E])
        wsum = sb("wsum", [P, QT])
        wsum1 = sb("wsum1", [P, QT])
        wrec = sb("wrec", [P, QT])
        wful = sb("wful", [P, QT, E])
        wsplit = sb("wsplit", [P, QT, 2 * E])
        w_ch = sb("w_ch", [P, TOK], F32R)
        raw = clip[:, 0:2].rearrange("p k c s -> p k (c s)")
        t_hi = k_st[:, 2, 0:4].rearrange("p (k n) s -> p k (n s)", k=2)
        t_lo = k_st[:, 2, 4:8].rearrange("p (k n) s -> p k (n s)", k=2)
        sel = k_st[:, 0, 0].rearrange("p (k m) -> p k m", k=2)
        relu, sq, act = (scan[:, 2 * n:2 * n + 2].rearrange("p k c s -> p k (c s)") for n in range(3))
        act_hi, act_lo = (q_st[:, 2, 4 * n:4 * n + 4].rearrange("p (k n) s -> p k (n s)", k=2) for n in range(2))
        res = f_sb[:].rearrange("p c (k s) -> p c k s", k=2)

        ld_in = [sem(f"ld_in{b}") for b in range(B)]
        ld_vec, ld_w, ld_gate = sem("ld_vec"), sem("ld_w"), sem("ld_gate")
        fill_ready, ld_fill = sem("fill_ready"), sem("ld_fill")
        st_qk = sem("st_qk")
        ld_stack = [sem(f"ld_stack{n}") for n in range(SLOTS)]
        ld_rows = [sem(f"ld_rows{n}") for n in range(SLOTS)]
        ld_raw = [sem(f"ld_raw{i}") for i in range(2)]
        st_out = sem("st_out")
        pool_const, dve_const, ident_ready, tile_no_ready = sem("pool_const"), sem("dve_const"), sem("ident_ready"), sem("tile_no_ready")
        tsum_ready, setup_exp, setup_step, decay_ready = sem("tsum_ready"), sem("setup_exp"), sem("setup_step"), sem("decay_ready")
        clip_ready, ex_ready, pool_pre, pool_sum = sem("clip_ready"), sem("ex_ready"), sem("pool_pre"), sem("pool_sum")
        fwd_ready, bwd_ready, numden_ready, den_ready = sem("fwd_ready"), sem("bwd_ready"), sem("numden_ready"), sem("den_ready")
        ln1_ready, lnsum1_ready, rec1_ready, hid1_ready = sem("ln1_ready"), sem("lnsum1_ready"), sem("rec1_ready"), sem("hid1_ready")
        misc_full = [sem(f"misc_full{i}") for i in range(2)]
        misc_free = [sem(f"misc_free{i}") for i in range(2)]
        qk_hi_ready, qk_lo_ready, v_ready = sem("qk_hi_ready"), sem("qk_lo_ready"), sem("v_ready")
        s_ready, max_ready, nmax_hi_ready, nmax_lo_ready = sem("s_ready"), sem("max_ready"), sem("nmax_hi_ready"), sem("nmax_lo_ready")
        t_ready, prob_ready, pv_ready, o_raw_ready = sem("t_ready"), sem("prob_ready"), sem("pv_ready"), sem("o_raw_ready")
        rsum_ready, o_tok_ready, o_ch_ready, x1_ready = sem("rsum_ready"), sem("o_tok_ready"), sem("o_ch_ready"), sem("x1_ready")
        clip2_ready, ex2_ready, lne2_ready, lnsum2_ready, rec2_ready = sem("clip2_ready"), sem("ex2_ready"), sem("lne2_ready"), sem("lnsum2_ready"), sem("rec2_ready")
        hid2_ready, hid_hi_ready, hid_lo_ready = sem("hid2_ready"), sem("hid_hi_ready"), sem("hid_lo_ready")
        gex_ready, route, wsplit_ready, w_ch_ready = sem("gex_ready"), sem("route"), sem("wsplit_ready"), sem("w_ch_ready")
        up_hi_ready, up_lo_ready, dn_hi_ready, dn_lo_ready = sem("up_hi_ready"), sem("up_lo_ready"), sem("dn_hi_ready"), sem("dn_lo_ready")
        sel_ready, h_ready, wb_ready, relu_ready = sem("sel_ready"), sem("h_ready"), sem("wb_ready"), sem("relu_ready")
        sq_ready, act_ready, act_hi_ready, act_lo_ready = sem("sq_ready"), sem("act_ready"), sem("act_hi_ready"), sem("act_lo_ready")
        down_done, res_ready = sem("down_done"), sem("res_ready")

        def slot(b, half):
            return (KC * b + half) % SLOTS

        def turn(b, half):
            return (KC * b + half) // SLOTS + 1

        def bank_s(n):
            return ps[:, n % 2, :].rearrange("p (t k) -> p t k", t=QT)

        def bank_t(n):
            return ps[:, 2 + n % 3, :].rearrange("p (t q) -> p t q", t=QT)

        bank_o = ps[:, 5, 0:S]
        jobs = [("v", 0), ("q", 0), ("k", 0)]
        for b in range(B):
            jobs += [("m", b, 0)]
            jobs += [("gate", b - 1)] if b > 0 else []
            jobs += [("v", b + 1)] if b + 1 < B else []
            jobs += [("m", b, 1)]
            jobs += [("q", b + 1), ("k", b + 1)] if b + 1 < B else []
            jobs += [("wt", b - 1)] if b > 0 else []
            jobs += [("ot", b, 0), ("ot", b, 1), ("oc", b), ("proj", b)]
        jobs += [("gate", B - 1), ("wt", B - 1)]
        job_no = {job: n for n, job in enumerate(jobs)}

        def job_bank(job):
            return ps[:, 6 + job_no[job] % 2, :]

        def job_begin(eng, job):
            n = job_no[job]
            if n >= 2:
                eng.wait_ge(misc_free[n % 2], n // 2)

        def job_sem(job):
            return misc_full[job_no[job] % 2]

        def job_wait(eng, job):
            n = job_no[job]
            eng.wait_ge(misc_full[n % 2], n // 2 + 1)

        def job_free(job):
            return misc_free[job_no[job] % 2]

        def bank_h(half):
            return ps[:, half, :]

        def bank_w(half):
            return ps[:, 6 + half, :]

        def bank_acc(oc, half):
            return ps[:, 2 + 2 * oc + half, :]

        def tok(b):
            return slice(b * S, (b + 1) * S)

        block = ctx.enter_context(nc.Block())

        @block.sync
        def _(sp):
            sp.dma_start(vec[:], vecs).then_inc(ld_vec, 16)
            sp.dma_start(cond_sb[:], cond.partition_broadcast(P)).then_inc(ld_vec, 16)
            for b in range(B):
                sp.dma_start(f_sb[:, :, tok(b)], fT[:, :, tok(b)]).then_inc(ld_in[b], 16)
                sp.dma_start(x_sb[:, :, tok(b)], xT[:, :, tok(b)]).then_inc(ld_in[b], 16)
                if b == 0:
                    sp.dma_start(wi[:], w_in).then_inc(ld_w, 16)
                    sp.dma_start(bvb[:], bv.partition_broadcast(P)).then_inc(ld_w, 16)
                    sp.dma_start(wo[:], w_out).then_inc(ld_w, 16)
                    sp.wait_ge(fill_ready, 2)
                    for st, r0, r1 in ((q_st, STACK, MAXROW), (k_st, STACK, MAXROW), (k_st, MAXROW, MAXROW + 2)):
                        sp.dma_start(st[r0:r1].rearrange("p n h s -> p (n h) s").bitcast(F32),
                                     fill[r0:r1].unsqueeze(1).broadcast_to([r1 - r0, SLOTS * HB, S])).then_inc(ld_fill, 16)
            sp.dma_start(gw[:], gate_w).then_inc(ld_gate, 16)
            sp.dma_start(gbb[:], gate_bias.partition_broadcast(P)).then_inc(ld_gate, 16)

            def store_qk(b):
                sp.wait_ge(qk_hi_ready, 4 * (b + 1))
                sp.wait_ge(qk_lo_ready, 4 * (b + 1))
                for w in range(4):
                    part = (qk_hi, qk_lo)[w % 2]
                    sp.dma_start(qk_dram[w, :, tok(b)].rearrange("(t p) s -> p t s", p=P),
                                 part[:, w // 2, :, :].bitcast(F32)).then_inc(st_qk, 16)

            def load_stack(b, half):
                n = slot(b, half)
                if turn(b, half) > 1:
                    sp.wait_ge(t_ready, HB * (KC * b + half - SLOTS + 1))
                for r in range(ROLE):
                    for st, w in ((q_st, r % 2), (k_st, 2 + r // 2)):
                        src = qk_dram[w, half * P:(half + 1) * P, tok(b)]
                        sp.dma_start(st[r * HD:(r + 1) * HD, n].bitcast(F32),
                                     src.rearrange("(h d) s -> d h s", d=HD)).then_inc(ld_stack[n], 16)

            def load_rows(b, half):
                for n, (src, ready) in enumerate(((nmax_hi, nmax_hi_ready), (nmax_lo, nmax_lo_ready))):
                    sp.wait_ge(ready, KC * b + half + 1)
                    dst = q_st[MAXROW + n:MAXROW + n + 1, slot(b, half)]
                    sp.dma_start(dst.rearrange("p h (t q) -> p (h t) q", t=QT).bitcast(F32),
                                 src[:, half, :].bitcast(F32)).then_inc(ld_rows[slot(b, half)], 16)

            store_qk(0)
            sp.wait_ge(st_qk, 64)
            load_stack(0, 0)
            load_stack(0, 1)
            for b in range(B):
                load_rows(b, 0)
                load_rows(b, 1)
                if b + 1 < B:
                    store_qk(b + 1)
                    sp.wait_ge(st_qk, 64 * (b + 2))
                    load_stack(b + 1, 0)
                    load_stack(b + 1, 1)

            sp.wait_ge(ex_ready, 4 * B)
            for i in range(2):
                sp.dma_start(raw[:, i, :], tiles[i]).then_inc(ld_raw[i], 16)
            with sp.Fori(0, NT // 2 - 1) as i:
                for k in range(2):
                    sp.wait_ge(dn_hi_ready, 2 * i + k + 1)
                    sp.wait_ge(dn_lo_ready, 2 * i + k + 1)
                    sp.dma_start(raw[:, k, :], tiles[2 * i + k + 2]).then_inc(ld_raw[k], 16)
            for oc in range(KC):
                for half in range(2):
                    sp.wait_ge(res_ready, 2 * oc + half + 1)
                    sp.dma_start(out[:, oc, half * HT:(half + 1) * HT], res[:, oc, half, :]).then_inc(st_out, 16)
            sp.wait_ge(st_out, 16 * 2 * KC)

        @block.gpsimd
        def _(pool):
            g = nc.gpsimd
            g.memset(ident[:], 0.0).then_inc(pool_const, 1)
            pool.wait_ge(pool_const, 1)
            g.affine_select(out=ident[:], in_=ident[:], compare_op=ALU.not_equal, fill=1.0, base=0,
                            pattern=[[-1, P]], channel_multiplier=1).then_inc(ident_ready, 1)
            g.iota(sel_i[:], pattern=[[-1, 2], [0, E]], base=0, channel_multiplier=1).then_inc(pool_const, 1)
            g.iota(tile_i[:], pattern=[[2, TILES]], base=0, channel_multiplier=0).then_inc(pool_const, 1)
            pool.wait_ge(pool_const, 3)
            g.tensor_copy(selval[:], sel_i[:]).then_inc(pool_const, 1)
            g.tensor_copy(tile_no[:], tile_i[:]).then_inc(tile_no_ready, 1)

            def products(b):
                f = f_sb[:, :, tok(b)]
                pool.wait_ge(ld_in[b], 32)
                pool.wait_ge(ex_ready, 4 * b + 3)
                if b > 0:
                    pool.wait_ge(bwd_ready, 8 * b)
                g.tensor_tensor(ekv[:], ex[:, 0], f, ALU.mult).then_inc(pool_pre, 1)
                for n in range(2):
                    g.tensor_tensor(gk[:, n], gk[:, n], ex[:, 0], ALU.subtract).then_inc(pool_pre, 1)
                for n in range(2):
                    pool.wait_ge(pool_pre, 5 * b + 2 + n)
                    g.tensor_tensor(gkv[:, n], gk[:, n], f, ALU.mult).then_inc(pool_pre, 1)

            def sums(b):
                for n in range(2):
                    pool.wait_ge(fwd_ready, 8 * b + 2 * n + 2)
                    pool.wait_ge(pool_pre, 5 * b + 4 + n)
                    g.tensor_tensor(scan[:, n], scan[:, n], gkv[:, n], ALU.add).then_inc(pool_sum, 1)
                for n in range(2):
                    pool.wait_ge(fwd_ready, 8 * b + 4 + 2 * n + 2)
                    g.tensor_tensor(scan[:, 2 + n], scan[:, 2 + n], gk[:, n], ALU.add).then_inc(pool_sum, 1)

            def add_logs1(b):
                pool.wait_ge(ln1_ready, 2 * (b + 1))
                g.tensor_tensor(den1[:], den1[:], ex[:, 3], ALU.add).then_inc(lnsum1_ready, 1)

            def add_logs2(b):
                pool.wait_ge(lne2_ready, 2 * (b + 1))
                g.tensor_tensor(den2[:, b % 2], den2[:, b % 2], ex2[:], ALU.add).then_inc(lnsum2_ready, 1)

            def split_hidden(b):
                pool.wait_ge(hid_hi_ready, b + 1)
                g.tensor_tensor(hid_lo[:, :, tok(b)], hid2[:], hid_hi[:, :, tok(b)].bitcast(F32),
                                ALU.subtract).then_inc(hid_lo_ready, 1)

            products(0)
            sums(0)
            add_logs1(0)
            for b in range(B):
                if b > 0:
                    add_logs2(b - 1)
                if b + 1 < B:
                    products(b + 1)
                if b > 0:
                    split_hidden(b - 1)
                if b + 1 < B:
                    sums(b + 1)
                    add_logs1(b + 1)
            add_logs2(B - 1)
            split_hidden(B - 1)

            def square(n, half):
                pool.wait_ge(relu_ready, n + 1)
                g.tensor_tensor(sq[:, half], relu[:, half], relu[:, half], ALU.mult).then_inc(sq_ready, 1)

            for half in range(2):
                square(half, half)
            with pool.Fori(1, NT) as t:
                for half in range(2):
                    pool.wait_ge(act_hi_ready, 2 * t + half - 1)
                    pool.wait_ge(act_lo_ready, 2 * t + half - 1)
                    square(2 * t + half, half)

        @block.scalar
        def _(sc):
            a = nc.scalar
            a.preload_act_table_set("natural_log_exp_and_others")
            sc.wait_ge(ld_vec, 32)
            for n, v in enumerate((V_W1, V_W2)):
                a.activation(dexp[:, n * KC:(n + 1) * KC], vec[:, v:v + KC], ACT.Exp).then_inc(setup_exp, 1)
            sc.wait_ge(setup_exp, 2)
            a.activation(dbase[:], dexp[:], ACT.Exp, scale=-1.0).then_inc(setup_exp, 1)
            sc.wait_ge(tsum_ready, 1)
            a.activation(tex[:], tsum[:], ACT.Exp, scale=-1.0).then_inc(setup_exp, 1)

            def exponentials(b):
                sc.wait_ge(clip_ready, 6 * (b + 1))
                if b > 0:
                    sc.wait_ge(pool_sum, 4 * b)
                    sc.wait_ge(bwd_ready, 8 * b)
                    sc.wait_ge(lnsum1_ready, b)
                for n in range(4):
                    a.activation(ex[:, n], clip[:, n], ACT.Exp, scale=1.0 if n < 3 else -1.0).then_inc(ex_ready, 1)
                sc.wait_ge(ex_ready, 4 * (b + 1))
                a.activation(ex[:, 3], ex[:, 3], ACT.Ln, bias=1.0).then_inc(ln1_ready, 1)

            def log_den(b):
                sc.wait_ge(den_ready, 2 * b + 1)
                a.activation(den1[:], den1[:], ACT.Ln).then_inc(ln1_ready, 1)

            def reciprocal1(b):
                sc.wait_ge(lnsum1_ready, b + 1)
                a.activation(den1[:], den1[:], ACT.Exp, scale=-1.0).then_inc(rec1_ready, 1)

            def evacuate_qk(b):
                sc.wait_ge(ld_vec, 32)
                if b > 0:
                    sc.wait_ge(st_qk, 64 * b)
                for w, v in enumerate((V_BQ, V_BK)):
                    job = ("qk"[w], b)
                    job_wait(sc, job)
                    for t in range(KC):
                        a.activation(qk_hi[:, w, t], job_bank(job)[:, t * S:(t + 1) * S], ACT.Identity,
                                     bias=vec[:, v + t:v + t + 1]).then_inc(qk_hi_ready, 1)

            def negate_max(b, half):
                job = ("m", b, half)
                job_wait(sc, job)
                if b > 0:
                    sc.wait_ge(ld_rows[slot(b - 1, half)], 32 * turn(b - 1, half))
                a.activation(nmax_hi[:, half], job_bank(job)[0:H, 0:P], ACT.Copy, scale=-1.0).then_inc(nmax_hi_ready, 1)

            def probabilities(b, half):
                for h in range(half * HB, (half + 1) * HB):
                    n = H * b + h
                    sc.wait_ge(t_ready, n + 1)
                    if n >= PRING:
                        sc.wait_ge(pv_ready, (n - PRING) // 4 + 1)
                    a.activation(prob[:, n % PRING], bank_t(n), ACT.Exp, scale=SCALE).then_inc(prob_ready, 1)
                    if h % 4 == 3 and h > half * HB + 3:
                        evacuate_o(b, h // 4 - 1)
                evacuate_o(b, (half + 1) * HB // 4 - 1)

            def evacuate_o(b, grp):
                sc.wait_ge(pv_ready, 4 * b + grp + 1)
                if b > 0:
                    n = job_no[("ot", b - 1, 1)]
                    sc.wait_ge(misc_full[n % 2], n // 2 + 1)
                a.activation(o_raw[:, grp], bank_o, ACT.Copy).then_inc(o_raw_ready, 1)

            def evacuate_o_ch(b):
                job_wait(sc, ("oc", b))
                if b > 0:
                    n = job_no[("proj", b - 1)]
                    sc.wait_ge(misc_full[n % 2], n // 2 + 1)
                a.activation(o_ch[:], job_bank(("oc", b)).rearrange("p (t q) -> p t q", t=KC), ACT.Copy).then_inc(o_ch_ready, 1)
                sc.wait_ge(o_ch_ready, b + 1)
                sc.sem_inc(job_free(("oc", b)), 1)

            def second_exp(b):
                sc.wait_ge(clip2_ready, b + 1)
                a.activation(ex2[:], ex2[:], ACT.Exp, scale=-1.0).then_inc(ex2_ready, 1)
                sc.wait_ge(den_ready, 2 * b + 2)
                a.activation(den2[:, b % 2], den2[:, b % 2], ACT.Ln).then_inc(lne2_ready, 1)
                sc.wait_ge(ex2_ready, b + 1)
                a.activation(ex2[:], ex2[:], ACT.Ln, bias=1.0).then_inc(lne2_ready, 1)

            def second_rec(b):
                sc.wait_ge(lnsum2_ready, b + 1)
                a.activation(den2[:, b % 2], den2[:, b % 2], ACT.Exp, scale=-1.0).then_inc(rec2_ready, 1)

            def round_hidden(b):
                sc.wait_ge(hid2_ready, b + 1)
                a.activation(hid_hi[:, :, tok(b)], hid2[:], ACT.Copy).then_inc(hid_hi_ready, 1)

            def gate_exp(b):
                job = ("gate", b)
                job_wait(sc, job)
                if b > 0:
                    sc.wait_ge(wsplit_ready, 2 * b)
                a.activation(gex[:], job_bank(job)[:, 0:QT * E].rearrange("p (t e) -> p t e", t=QT), ACT.Exp,
                             scale=-1.0).then_inc(gex_ready, 1)
                sc.wait_ge(gex_ready, b + 1)
                sc.sem_inc(job_free(job), 1)

            def evacuate_w(b):
                job_wait(sc, ("wt", b))
                a.activation(w_ch[:, tok(b)], job_bank(("wt", b))[:, 0:S], ACT.Copy).then_inc(w_ch_ready, 1)
                sc.wait_ge(w_ch_ready, b + 1)
                sc.sem_inc(job_free(("wt", b)), 1)

            exponentials(0)
            log_den(0)
            reciprocal1(0)
            evacuate_qk(0)
            for b in range(B):
                if b > 0:
                    second_exp(b - 1)
                if b + 1 < B:
                    exponentials(b + 1)
                if b > 0:
                    second_rec(b - 1)
                    round_hidden(b - 1)
                negate_max(b, 0)
                if b > 0:
                    gate_exp(b - 1)
                probabilities(b, 0)
                if b + 1 < B:
                    log_den(b + 1)
                    reciprocal1(b + 1)
                negate_max(b, 1)
                if b + 1 < B:
                    evacuate_qk(b + 1)
                probabilities(b, 1)
                if b > 0:
                    evacuate_w(b - 1)
                evacuate_o_ch(b)
            second_exp(B - 1)
            second_rec(B - 1)
            round_hidden(B - 1)
            gate_exp(B - 1)

            def split_up(k):
                sc.wait_ge(ld_raw[k], 16)
                a.activation(t_hi[:, k, 0:C], raw[:, k, 0:C], ACT.Copy).then_inc(up_hi_ready, 1)

            def split_down(k):
                a.activation(t_hi[:, k, C:2 * C], raw[:, k, C:2 * C], ACT.Copy).then_inc(dn_hi_ready, 1)

            def rectify(n, half):
                sc.wait_ge(h_ready, n + 1)
                a.activation(relu[:, half], bank_h(half), ACT.Relu).then_inc(relu_ready, 1)

            def round_act(n, half):
                sc.wait_ge(act_ready, n + 1)
                a.activation(act_hi[:, half], act[:, half], ACT.Copy).then_inc(act_hi_ready, 1)

            split_up(0)
            evacuate_w(B - 1)

            split_up(1)
            split_down(0)
            for half in range(2):
                rectify(half, half)
            for half in range(2):
                round_act(half, half)

            def tile(t, k, split=True, up_wait=None):
                if split:
                    sc.wait_ge(ld_raw[1 - k], up_wait)
                    sc.wait_ge(h_ready, 2 * t)
                    a.activation(t_hi[:, 1 - k, 0:C], raw[:, 1 - k, 0:C], ACT.Copy).then_inc(up_hi_ready, 1)
                if not isinstance(t, int) or t > 1:
                    sc.wait_ge(down_done, 2 * (t - 1))
                split_down(k)
                for half in range(2):
                    sc.wait_ge(sq_ready, 2 * (t - 1) + half + 1)
                    rectify(2 * t + half, half)
                for half in range(2):
                    sc.wait_ge(down_done, 2 * (t - 1) + half + 1)
                    round_act(2 * t + half, half)

            tile(1, 1, up_wait=32)
            with sc.Fori(1, NT // 2 - 1) as i:
                tile(2 * i, 0, up_wait=16 * i + 16)
                tile(2 * i + 1, 1, up_wait=16 * i + 32)
            tile(NT - 2, 0, up_wait=16 * (NT // 2))
            tile(NT - 1, 1, split=False)

        @block.vector
        def _(dve):
            v = nc.vector
            TT = v.tensor_tensor
            v.memset(fill[0:MAXROW], 0.0).then_inc(fill_ready, 1)
            v.memset(fill[MAXROW:P], 1.0).then_inc(fill_ready, 1)
            v.memset(v_aug[:, :, :, :, HD:32], 1.0).then_inc(dve_const, 1)
            v.memset(gsum[:, :, G:G + 4], NONE).then_inc(dve_const, 1)
            v.memset(masked[:, :, E:E + 2], NONE).then_inc(dve_const, 1)
            dve.wait_ge(pool_const, 4)
            v.tensor_scalar(selval[E:P, :], selval[E:P, :], float(-E), None, ALU.add).then_inc(dve_const, 1)

            def clips(b):
                if b == 0:
                    dve.wait_ge(ld_vec, 32)
                dve.wait_ge(ld_in[b], 32)
                if b > 0:
                    dve.wait_ge(ex_ready, 4 * b)
                    dve.wait_ge(pool_sum, 4 * b)
                f = f_sb[:, :, tok(b)]
                v.tensor_scalar(clip[:, 0], f, 30.0, None, ALU.min).then_inc(clip_ready, 1)
                for n, u in enumerate((V_U1, V_U2)):
                    for c in range(KC):
                        v.tensor_scalar(clip[:, 1 + n, c], f[:, c], vec[:, u + c:u + c + 1], 30.0,
                                        ALU.add, ALU.min).then_inc(clip_ready, 1)
                v.tensor_scalar(clip[:, 3], x_sb[:, :, tok(b)], -41.0, None, ALU.max).then_inc(clip_ready, 1)

            clips(0)
            v.tensor_reduce(tsum[:], cond_sb[:], AX_X, ALU.add).then_inc(tsum_ready, 1)
            dve.wait_ge(setup_exp, 4)
            v.tensor_scalar(tden[:], tex[:], 1.0, None, ALU.add).then_inc(setup_step, 1)
            dve.wait_ge(setup_step, 1)
            v.reciprocal(tf[:], tden[:]).then_inc(setup_step, 1)
            dve.wait_ge(setup_step, 2)
            v.tensor_scalar(thalf[:], tf[:], 0.5, 0.5, ALU.mult, ALU.add).then_inc(setup_step, 1)
            v.tensor_scalar(cfac[:], tf[:], 0.2, 0.8, ALU.mult, ALU.add).then_inc(setup_step, 1)
            dve.wait_ge(setup_step, 4)
            for n in range(2 * KC):
                v.tensor_scalar(decay[:, n], thalf[:], dbase[:, n:n + 1], None, ALU.mult).then_inc(decay_ready, 1)

            def scans(b, between=lambda: None):
                if b == 0:
                    dve.wait_ge(decay_ready, 2 * KC)
                for back in range(2):
                    for which in range(2):
                        if back == 1 and which == 0:
                            between()
                        if back == 0:
                            dve.wait_ge(pool_pre, 5 * b + 1) if which == 0 else dve.wait_ge(ex_ready, 4 * b + 1)
                            if b > 0:
                                dve.wait_ge(numden_ready, 4 * b)
                        for n in range(2):
                            for c in range(KC):
                                src = (ekv[:, c], ex[:, 0, c])[which]
                                dst = scan[:, 4 * back + 2 * which + n, c]
                                if back:
                                    src, dst = src[:, ::-1], dst[:, ::-1]
                                v.tensor_tensor_scan(dst, decay[:, n * KC + c, b:b + 1].broadcast_to([P, S]), src, 0.0,
                                                     ALU.mult, ALU.add).then_inc((fwd_ready, bwd_ready)[back], 1)

            def num_den(b):
                if b > 0:
                    dve.wait_ge(hid1_ready, b)
                if b > 1:
                    dve.wait_ge(hid2_ready, b - 1)
                dst = ((num1[:], num2[:, b % 2]), (den1[:], den2[:, b % 2]))
                for which in range(2):
                    for n in range(2):
                        dve.wait_ge(pool_sum, 4 * b + 2 * which + n + 1)
                        dve.wait_ge(bwd_ready, 8 * b + 4 * which + 2 * n + 2)
                        row = 2 * which + n
                        TT(dst[which][n], scan[:, row], scan[:, 4 + row], ALU.add).then_inc(numden_ready, 1)
                for n in range(2):
                    dve.wait_ge(numden_ready, 4 * b + 3 + n)
                    v.tensor_scalar(dst[1][n], dst[1][n], 1e-8, None, ALU.max).then_inc(den_ready, 1)

            def hidden1(b):
                dve.wait_ge(rec1_ready, b + 1)
                if b > 0:
                    job_wait(dve, ("k", b - 1))
                v.scalar_tensor_tensor(hid1[:], num1[:], cfac[:, b:b + 1], den1[:], ALU.mult,
                                       ALU.mult).then_inc(hid1_ready, 1)

            def split_qk(b):
                for w, u in enumerate((V_BQ, V_BK)):
                    job = ("qk"[w], b)
                    dve.wait_ge(qk_hi_ready, 4 * b + 2 * w + 2)
                    for t in range(KC):
                        last = v.scalar_tensor_tensor(qk_lo[:, w, t], job_bank(job)[:, t * S:(t + 1) * S],
                                                      vec[:, u + t:u + t + 1], qk_hi[:, w, t].bitcast(F32), ALU.add,
                                                      ALU.subtract).then_inc(qk_lo_ready, 1)
                    dve.wait_ge(qk_lo_ready, 4 * b + 2 * w + 2)
                    dve.sem_inc(job_free(job), 1)

            def add_v_bias(b):
                job = ("v", b)
                job_wait(dve, job)
                for t in range(QT):
                    if b > 1 and t == 0:
                        dve.wait_ge(pv_ready, 4 * (b - 1))
                    src = job_bank(job)[:, t * C:(t + 1) * C].rearrange("p (h d) -> p h d", d=HD)
                    TT(v_aug[:, b % 2, t, :, 0:HD], src, bvb[:].rearrange("p (h d) -> p h d", d=HD),
                       ALU.add).then_inc(v_ready, 1)
                dve.wait_ge(v_ready, QT * (b + 1))
                dve.sem_inc(job_free(job), 1)

            def maximum(b, h):
                n = H * b + h
                dve.wait_ge(s_ready, n + 1)
                if b > 1 and h == 0:
                    n2 = job_no[("m", b - 2, 1)]
                    dve.wait_ge(misc_full[n2 % 2], n2 // 2 + 1)
                v.tensor_reduce(mx[:, b % 2, h], bank_s(n), AX_X, ALU.max).then_inc(max_ready, 1)

            def low_max(b, half):
                job = ("m", b, half)
                dve.wait_ge(nmax_hi_ready, KC * b + half + 1)
                v.scalar_tensor_tensor(nmax_lo[:, half], job_bank(job)[0:H, 0:P], -1.0, nmax_hi[:, half].bitcast(F32),
                                       ALU.mult, ALU.subtract).then_inc(nmax_lo_ready, 1)
                dve.wait_ge(nmax_lo_ready, KC * b + half + 1)
                dve.sem_inc(job_free(job), 1)

            def normalise(b):
                for qt in range(QT):
                    job = ("ot", b, qt)
                    job_wait(dve, job)
                    src = job_bank(job).rearrange("p (h c) -> p h c", c=32)
                    if b > 0 and qt == 0:
                        n = job_no[("oc", b - 1)]
                        dve.wait_ge(misc_full[n % 2], n // 2 + 1)
                    v.reciprocal(rsum[:, qt], src[:, :, HD]).then_inc(rsum_ready, 1)
                    dve.wait_ge(rsum_ready, QT * b + qt + 1)
                    TT(o_tok[:, qt], src[:, :, 0:HD], rsum[:, qt].unsqueeze(2).broadcast_to([P, H, HD]),
                       ALU.mult).then_inc(o_tok_ready, 1)
                    dve.wait_ge(o_tok_ready, QT * b + qt + 1)
                    dve.sem_inc(job_free(job), 1)

            def residual(b):
                job = ("proj", b)
                job_wait(dve, job)
                for c in range(KC):
                    v.scalar_tensor_tensor(x1[:, c, tok(b)], job_bank(job)[:, c * S:(c + 1) * S],
                                           vec[:, V_BP + c:V_BP + c + 1], x_sb[:, c, tok(b)], ALU.add,
                                           ALU.add).then_inc(x1_ready, 1)
                dve.wait_ge(x1_ready, KC * (b + 1))
                dve.sem_inc(job_free(job), 1)
                if b > 0:
                    dve.wait_ge(lnsum2_ready, b)
                v.tensor_scalar(ex2[:], x1[:, :, tok(b)], -41.0, None, ALU.max).then_inc(clip2_ready, 1)

            def hidden2(b):
                dve.wait_ge(rec2_ready, b + 1)
                if b > 0:
                    dve.wait_ge(hid_hi_ready, b)
                    dve.wait_ge(hid_lo_ready, b)
                    n = job_no[("gate", b - 1)]
                    dve.wait_ge(misc_full[n % 2], n // 2 + 1)
                v.scalar_tensor_tensor(hid2[:], num2[:, b % 2], cfac[:, b:b + 1], den2[:, b % 2], ALU.mult,
                                       ALU.mult).then_inc(hid2_ready, 1)

            def router(b):
                count = [b * ROUTE_STEPS]

                def step(ins):
                    ins.then_inc(route, 1)
                    count[0] += 1
                    dve.wait_ge(route, count[0])

                if b == 0:
                    dve.wait_ge(ld_gate, 32)
                dve.wait_ge(gex_ready, b + 1)
                step(v.tensor_scalar(gden[:], gex[:], 1.0, None, ALU.add))
                step(v.reciprocal(score[:], gden[:]))
                for t in range(QT):
                    step(TT(sbias[:, t], score[:, t].rearrange("p (g e) -> p g e", g=G),
                            gbb[:].rearrange("p (g e) -> p g e", g=G), ALU.add))
                pairs = sbias[:].rearrange("p t g (a c) -> p (t g) a c", c=2)
                step(TT(pmax[:], pairs[:, :, :, 0], pairs[:, :, :, 1], ALU.max))
                step(TT(pmin[:], pairs[:, :, :, 0], pairs[:, :, :, 1], ALU.min))
                for best, low, nbest, mid, nlow, nsec, w in ((pmax, pmin, qmax, qmid, qlow, qsec, 2),
                                                             (qmax, qsec, fmax, fmid, flow, fsec, 1)):
                    step(TT(nbest[:], best[:, :, 0:w], best[:, :, w:2 * w], ALU.max))
                    step(TT(mid[:], best[:, :, 0:w], best[:, :, w:2 * w], ALU.min))
                    step(TT(nlow[:], low[:, :, 0:w], low[:, :, w:2 * w], ALU.max))
                    step(TT(nsec[:], mid[:], nlow[:], ALU.max))
                step(TT(gsum[:, :, 0:G], fmax[:, :, 0].rearrange("p (t g) -> p t g", t=QT),
                        fsec[:, :, 0].rearrange("p (t g) -> p t g", t=QT), ALU.add))
                for t in range(QT):
                    step(v.max(gtop[:, t], gsum[:, t, 0:G]))
                step(v.memset(gtop[:, :, GT:8], NONE))
                for t in range(QT):
                    step(v.match_replace(grep[:, t], gtop[:, t], gsum[:, t], BIG))
                step(v.tensor_scalar(gpen[:], grep[:, :, 0:G], BIG, -BIG, ALU.is_lt, ALU.mult))
                for t in range(QT):
                    step(TT(masked[:, t, 0:E].rearrange("p (g e) -> p g e", g=G), sbias[:, t],
                            gpen[:, t].unsqueeze(2).broadcast_to([P, G, EG]), ALU.add))
                for t in range(QT):
                    step(v.max(etop[:, t], masked[:, t, 0:E]))
                step(v.memset(etop[:, :, TOPK:8], NONE))
                for t in range(QT):
                    step(v.match_replace(erep[:, t], etop[:, t], masked[:, t], BIG))
                step(v.scalar_tensor_tensor(wsel[:], erep[:, :, 0:E], BIG, score[:], ALU.is_ge, ALU.mult))
                step(v.tensor_reduce(wsum[:], wsel[:], AX_X, ALU.add))
                step(v.tensor_scalar(wsum1[:], wsum[:], 1e-20, None, ALU.add))
                step(v.reciprocal(wrec[:], wsum1[:]))
                for t in range(QT):
                    step(v.tensor_scalar(wful[:, t], wsel[:, t], wrec[:, t:t + 1], 2.5, ALU.mult, ALU.mult))
                assert count[0] == (b + 1) * ROUTE_STEPS, count[0]
                if b > 0:
                    n = job_no[("wt", b - 1)]
                    dve.wait_ge(misc_full[n % 2], n // 2 + 1)
                v.tensor_copy(wsplit[:, :, 0:E].bitcast(F32R), wful[:]).then_inc(wsplit_ready, 1)
                dve.wait_ge(wsplit_ready, 2 * b + 1)
                TT(wsplit[:, :, E:2 * E].bitcast(F32R), wful[:], wsplit[:, :, 0:E], ALU.subtract).then_inc(wsplit_ready, 1)

            ROUTE_STEPS = 34

            scans(0)
            num_den(0)
            hidden1(0)
            clips(1)
            dve.wait_ge(ld_w, 48)
            add_v_bias(0)
            split_qk(0)
            for b in range(B):
                for h in range(HB):
                    maximum(b, h)
                    if b > 0 and h == 4:
                        hidden2(b - 1)
                if b + 1 < B:
                    scans(b + 1, between=lambda: low_max(b, 0))
                    num_den(b + 1)
                for h in range(HB, H):
                    maximum(b, h)
                    if b + 1 == B and h == HB + 1:
                        low_max(b, 0)
                    if b + 1 < B and h == H - 3:
                        hidden1(b + 1)
                if b + 1 < B:
                    add_v_bias(b + 1)
                low_max(b, 1)
                if b + 1 < B:
                    split_qk(b + 1)
                if b > 0:
                    router(b - 1)
                if b + 2 < B:
                    clips(b + 2)
                normalise(b)
                residual(b)
            hidden2(B - 1)
            router(B - 1)

            def split_up(k):
                TT(t_lo[:, k, 0:C], raw[:, k, 0:C], t_hi[:, k, 0:C].bitcast(F32), ALU.subtract).then_inc(up_lo_ready, 1)

            def split_down(k):
                TT(t_lo[:, k, C:2 * C], raw[:, k, C:2 * C], t_hi[:, k, C:2 * C].bitcast(F32),
                   ALU.subtract).then_inc(dn_lo_ready, 1)

            def select(t, k):
                v.tensor_scalar(sel[:, k], selval[:], tile_no[:, bass.ds(t, 1)], None, ALU.is_equal).then_inc(sel_ready, 1)

            def gated(n, half):
                dve.wait_ge(sq_ready, n + 1)
                dve.wait_ge(wb_ready, n + 1)
                TT(act[:, half], sq[:, half], bank_w(half), ALU.mult).then_inc(act_ready, 1)

            def shared(n, half):
                dve.wait_ge(sq_ready, n + 1)
                v.tensor_copy(act[:, half], sq[:, half]).then_inc(act_ready, 1)

            def low_act(n, half):
                dve.wait_ge(act_hi_ready, n + 1)
                TT(act_lo[:, half], act[:, half], act_hi[:, half].bitcast(F32), ALU.subtract).then_inc(act_lo_ready, 1)

            dve.wait_ge(tile_no_ready, 1)
            dve.wait_ge(dve_const, 4)
            dve.wait_ge(up_hi_ready, 1)
            split_up(0)
            select(0, 0)
            dve.wait_ge(up_hi_ready, 2)
            split_up(1)
            select(1, 1)
            dve.wait_ge(dn_hi_ready, 1)
            split_down(0)
            for half in range(2):
                gated(half, half)
                low_act(half, half)

            def tile(t, k, mult=gated, split=True, pick=True):
                if split:
                    dve.wait_ge(up_hi_ready, t + 2)
                    split_up(1 - k)
                if pick:
                    dve.wait_ge(wb_ready, 2 * t)
                    select(t + 1, 1 - k)
                dve.wait_ge(dn_hi_ready, t + 1)
                split_down(k)
                for half in range(2):
                    mult(2 * t + half, half)
                    dve.wait_ge(down_done, 2 * (t - 1) + half + 1)
                    low_act(2 * t + half, half)

            tile(1, 1)
            with dve.Fori(1, TILES // 2 - 1) as i:
                tile(2 * i, 0)
                tile(2 * i + 1, 1)
            tile(TILES - 2, 0)
            tile(TILES - 1, 1, pick=False)
            tile(TILES, 0, mult=shared, pick=False)
            tile(TILES + 1, 1, mult=shared, split=False, pick=False)
            dve.wait_ge(down_done, 2 * NT)
            for oc in range(KC):
                for half in range(2):
                    TT(res[:, oc, half], bank_acc(oc, half), x1[:, oc, half * HT:(half + 1) * HT],
                       ALU.add).then_inc(res_ready, 1)

        @block.tensor
        def _(pe):
            mm = nc.tensor.matmul

            def project(b, names):
                pe.wait_ge(hid1_ready, b + 1)
                for name in names:
                    job = (name, b)
                    job_begin(pe, job)
                    w = "qkv".index(name) * C
                    for t in range(KC):
                        for c in range(KC):
                            weights, tokens = wi[:, c, w + t * P:w + (t + 1) * P], hid1[:, c, :]
                            if name == "v":
                                weights, tokens = hid1[:, c, t * P:(t + 1) * P], wi[:, c, w:w + C]
                            last = mm(job_bank(job)[:, t * S:(t + 1) * S], weights, tokens, start=(c == 0),
                                      stop=(c == KC - 1))
                    last.then_inc(job_sem(job), 1)

            def scores(b, h):
                n = H * b + h
                if h % HB == 0:
                    pe.wait_ge(ld_stack[slot(b, h // HB)], 16 * 2 * ROLE * turn(b, h // HB))
                if n >= 2:
                    pe.wait_ge(max_ready, n - 1)
                for qt in range(QT):
                    last = mm(bank_s(n)[:, qt], q_st[0:MAXROW, slot(b, h // HB), h % HB, qt * P:(qt + 1) * P],
                              k_st[0:MAXROW, slot(b, h // HB), h % HB, :], start=True, stop=True)
                last.then_inc(s_ready, 1)

            def turn_max(b, half):
                job = ("m", b, half)
                job_begin(pe, job)
                pe.wait_ge(max_ready, H * b + HB * (half + 1))
                nc.tensor.transpose(job_bank(job)[0:H, 0:P],
                                    mx[:, b % 2, half * HB:(half + 1) * HB].rearrange("p h t -> p (h t)"),
                                    ident[:]).then_inc(job_sem(job), 1)

            def shifted_scores(b, h):
                n = H * b + h
                if h % HB == 0:
                    pe.wait_ge(ld_rows[slot(b, h // HB)], 32 * turn(b, h // HB))
                if n >= 3:
                    pe.wait_ge(prob_ready, n - 2)
                for kt in range(QT):
                    last = mm(bank_t(n)[:, kt], k_st[0:MAXROW + 2, slot(b, h // HB), h % HB, kt * P:(kt + 1) * P],
                              q_st[0:MAXROW + 2, slot(b, h // HB), h % HB, :], start=True, stop=True)
                last.then_inc(t_ready, 1)

            def values(b, grp):
                if 4 * b + grp > 0:
                    pe.wait_ge(o_raw_ready, 4 * b + grp)
                pe.wait_ge(v_ready, QT * (b + 1))
                pe.wait_ge(prob_ready, H * b + 4 * grp + 4)
                for kt in range(QT):
                    for j in range(4):
                        h = 4 * grp + j
                        last = mm(bank_o[32 * j:32 * j + 32, :], v_aug[:, b % 2, kt, h, :],
                                  prob[:, (H * b + h) % PRING, kt, :], start=(kt == 0), stop=(kt == QT - 1))
                last.then_inc(pv_ready, 1)

            def turn_out(b):
                pe.wait_ge(o_raw_ready, 4 * (b + 1))
                for qt in range(QT):
                    job = ("ot", b, qt)
                    job_begin(pe, job)
                    for grp in range(4):
                        last = nc.tensor.transpose(job_bank(job)[:, grp * P:(grp + 1) * P],
                                                   o_raw[:, grp, qt * P:(qt + 1) * P], ident[:])
                    last.then_inc(job_sem(job), 1)
                job = ("oc", b)
                job_begin(pe, job)
                pe.wait_ge(o_tok_ready, QT * (b + 1))
                for c in range(KC):
                    for qt in range(QT):
                        last = nc.tensor.transpose(job_bank(job)[:, c * S + qt * P:c * S + (qt + 1) * P],
                                                   o_tok[:, qt, c * HB:(c + 1) * HB].rearrange("p h d -> p (h d)"), ident[:])
                last.then_inc(job_sem(job), 1)
                job = ("proj", b)
                job_begin(pe, job)
                pe.wait_ge(o_ch_ready, b + 1)
                for t in range(KC):
                    for c in range(KC):
                        last = mm(job_bank(job)[:, t * S:(t + 1) * S], wo[:, c, t * P:(t + 1) * P], o_ch[:, c, :],
                                  start=(c == 0), stop=(c == KC - 1))
                last.then_inc(job_sem(job), 1)

            def gate(b):
                job = ("gate", b)
                job_begin(pe, job)
                pe.wait_ge(ld_gate, 32)
                pe.wait_ge(hid2_ready, b + 1)
                for t in range(QT):
                    for c in range(KC):
                        last = mm(job_bank(job)[:, t * E:(t + 1) * E], hid2[:, c, t * P:(t + 1) * P], gw[:, c, :],
                                  start=(c == 0), stop=(c == KC - 1))
                last.then_inc(job_sem(job), 1)

            def turn_weights(b):
                job = ("wt", b)
                job_begin(pe, job)
                pe.wait_ge(wsplit_ready, 2 * (b + 1))
                for t in range(QT):
                    last = nc.tensor.transpose(job_bank(job)[:, t * P:(t + 1) * P], wsplit[:, t], ident[:])
                last.then_inc(job_sem(job), 1)

            pe.wait_ge(ld_w, 48)
            project(0, "vqk")
            pe.wait_ge(ident_ready, 1)
            pe.wait_ge(dve_const, 1)
            pe.wait_ge(ld_fill, 48)
            for b in range(B):
                for h in range(HB):
                    scores(b, h)
                turn_max(b, 0)
                if b > 0:
                    gate(b - 1)
                scores(b, HB)
                scores(b, HB + 1)
                for h in range(HB):
                    shifted_scores(b, h)
                    if h == 5:
                        values(b, 0)
                values(b, 1)
                for h in range(HB + 2, H):
                    scores(b, h)
                if b + 1 < B:
                    project(b + 1, "v")
                turn_max(b, 1)
                if b + 1 < B:
                    project(b + 1, "qk")
                for h in range(HB, H):
                    shifted_scores(b, h)
                    if h == HB + 5:
                        values(b, 2)
                values(b, 3)
                if b > 0:
                    turn_weights(b - 1)
                turn_out(b)
            gate(B - 1)
            turn_weights(B - 1)

            def up(t, k, half, wb=True):
                for c in range(KC):
                    w_hi, w_lo = (w[:, k, c * P:(c + 1) * P] for w in (t_hi, t_lo))
                    x_hi, x_lo = (x[:, c, half * HT:(half + 1) * HT] for x in (hid_hi, hid_lo))
                    mm(bank_h(half), w_hi, x_hi, start=(c == 0), stop=False)
                    mm(bank_h(half), w_hi, x_lo, start=False, stop=False)
                    last = mm(bank_h(half), w_lo, x_hi, start=False, stop=(c == KC - 1))
                last.then_inc(h_ready, 1)
                if wb:
                    mm(bank_w(half), sel[:, k], w_ch[:, half * HT:(half + 1) * HT], start=True,
                       stop=True).then_inc(wb_ready, 1)

            def down(k, half, first=False, final=False):
                for oc in range(KC):
                    w_hi, w_lo = (w[:, k, C + oc * P:C + (oc + 1) * P] for w in (t_hi, t_lo))
                    acc = bank_acc(oc, half)
                    mm(acc, w_hi, act_hi[:, half], start=first, stop=False, skip_group_check=True)
                    mm(acc, w_hi, act_lo[:, half], start=False, stop=False, skip_group_check=True)
                    last = mm(acc, w_lo, act_hi[:, half], start=False, stop=final, skip_group_check=True)
                last.then_inc(down_done, 1)

            def step(t, k, wb=True, first=False):
                pe.wait_ge(up_lo_ready, t + 1)
                if wb:
                    pe.wait_ge(sel_ready, t + 1)
                for half in range(2):
                    pe.wait_ge(relu_ready, 2 * (t - 1) + half + 1)
                    if wb:
                        pe.wait_ge(act_ready, 2 * (t - 1) + half + 1)
                    up(t, k, half, wb)
                pe.wait_ge(dn_lo_ready, t)
                for half in range(2):
                    pe.wait_ge(act_lo_ready, 2 * (t - 1) + half + 1)
                    down(1 - k, half, first)

            pe.wait_ge(hid_lo_ready, B)
            pe.wait_ge(hid_hi_ready, B)
            pe.wait_ge(w_ch_ready, B)
            pe.wait_ge(up_lo_ready, 1)
            pe.wait_ge(sel_ready, 1)
            for half in range(2):
                up(0, 0, half)
            step(1, 1, first=True)
            with pe.Fori(1, TILES // 2) as i:
                step(2 * i, 0)
                step(2 * i + 1, 1)
            step(TILES, 0, wb=False)
            step(TILES + 1, 1, wb=False)
            pe.wait_ge(dn_lo_ready, NT)
            for half in range(2):
                pe.wait_ge(act_lo_ready, 2 * (NT - 1) + half + 1)
                down(1, half, final=True)


def kernel(**inputs):
    import numpy as np
    import concourse.bacc as bacc
    from concourse.bass_utils import run_bass_kernel_spmd

    def arr(name):
        return np.asarray(inputs[name])

    def chunks(a):
        return np.ascontiguousarray(a.reshape(KC, P, -1).transpose(1, 0, 2))

    x, f = arr("x"), arr("fside_BxSxS_0")
    wqkv = arr("L0_attn_Wqkv").reshape(H, 3, HD, C).transpose(1, 0, 2, 3).reshape(3 * C, C)
    bqkv = arr("L0_attn_bqkv").reshape(H, 3, HD).transpose(1, 0, 2).reshape(3, C)
    cols = [arr("L0_cond_w"), arr("L0_cond_u"), arr("L0_cond2_w"), arr("L0_cond2_u"), bqkv[0], bqkv[1],
            arr("L0_attn_bproj")]
    up = np.concatenate([arr("L0_ffn_w1").reshape(E * I, C), arr("L0_ffn_shared_up")])
    down = np.concatenate([arr("L0_ffn_w2").transpose(0, 2, 1).reshape(E * I, C), arr("L0_ffn_shared_down").T])
    up = up.reshape(NT, P, KC, P).transpose(0, 3, 2, 1).reshape(NT, P, C)
    arrays = {
        "xT": chunks(x.reshape(TOK, C).T),
        "fT": chunks(f.reshape(TOK, C).T),
        "cond": arr("cond_512"),
        "vecs": np.concatenate([v.reshape(KC, P).T for v in cols], axis=1),
        "w_in": chunks(wqkv.T),
        "w_out": chunks(arr("L0_attn_Wproj").T),
        "gate_w": chunks(arr("L0_ffn_gate_w").T),
        "bv": bqkv[2],
        "gate_bias": arr("L0_ffn_gate_bias"),
        "tiles": np.concatenate([up, down.reshape(NT, P, C)], axis=2),
    }
    arrays = {f"in_{n}": np.ascontiguousarray(a) for n, a in arrays.items()}
    nc = bacc.Bacc("TRN2", target_bir_lowering=False, num_devices=1)
    args = [nc.dram_tensor(n, a.shape, mybir.dt.from_np(a.dtype), kind="ExternalInput").ap() for n, a in arrays.items()]
    out = nc.dram_tensor("out", (P, KC, TOK), F32, kind="ExternalOutput").ap()
    bass_adaln_attn_ffn(nc, *args, out)
    r = run_bass_kernel_spmd(nc, [arrays], core_ids=[0])
    y = r.results[0]["out"]
    return np.ascontiguousarray(y.transpose(2, 1, 0).reshape(B, S, C))
```

```python
from contextlib import ExitStack

import concourse.bass as bass
from concourse import mybir

P = 128
B, S, C = 4, 256, 256
TOK = B * S
KC = C // P
H, HD = 16, 16
HB = H // KC
QT = S // P
E, I = 64, 64
G, GT, TOPK = 8, 4, 6
EG = E // G
TILES = E * I // P
SHARED = 256 // P
NT = TILES + SHARED
TD = 64
ROLE = 4
STACK = ROLE * HD
MAXROW = 96
HT = 512
SCALE = float(HD) ** 0.5
SLOTS = 3
PRING = 8
BIG = 1.0e30
NONE = -3.0e38

F32 = mybir.dt.float32
F32R = mybir.dt.float32r
I32 = mybir.dt.int32
ALU = mybir.AluOpType
ACT = mybir.ActivationFunctionType
AX_X = mybir.AxisListType.X

V_W1, V_U1, V_W2, V_U2, V_BQ, V_BK, V_BP = (KC * n for n in range(7))
NVEC = 7 * KC


def bass_adaln_attn_ffn(nc, xT, fT, cond, vecs, w_in, w_out, gate_w, bv, gate_bias, tiles, out):
    qk_dram = nc.dram_tensor("qk_split", (2, B, KC, 2, HD, HB * S), F32, kind="Internal").ap()

    with ExitStack() as ctx:
        def sb(name, shape, dt=F32):
            return ctx.enter_context(nc.sbuf_tensor(name, shape, dt))

        def sem(name):
            return ctx.enter_context(nc.semaphore(name))

        ps = ctx.enter_context(nc.psum_tensor("ps", [P, 8, 512], F32))

        x_sb = sb("x_sb", [P, KC, TOK])
        f_sb = sb("f_sb", [P, KC, TOK])
        vec = sb("vec", [P, NVEC])
        cond_sb = sb("cond_sb", [P, B, TD])
        wi = sb("wi", [P, KC, 3 * C])
        wo = sb("wo", [P, KC, C])
        gw = sb("gw", [P, KC, E])
        bvb = sb("bvb", [P, C])
        gbb = sb("gbb", [P, E])
        ident = sb("ident", [P, P])
        selval = sb("selval", [P, P])
        sel_i = sb("sel_i", [P, P], I32)
        tile_i = sb("tile_i", [P, TILES], I32)
        tile_no = sb("tile_no", [P, TILES])
        tsum = sb("tsum", [P, B])
        tex = sb("tex", [P, B])
        tden = sb("tden", [P, B])
        tf = sb("tf", [P, B])
        thalf = sb("thalf", [P, B])
        cfac = sb("cfac", [P, B])
        dexp = sb("dexp", [P, 2 * KC])
        dbase = sb("dbase", [P, 2 * KC])
        decay = sb("decay", [P, 2 * KC, B])
        clip = sb("clip", [P, 4, KC, S])
        gkv = clip[:, 0:2]
        ex = sb("ex", [P, 4, KC, S])
        gk = ex[:, 1:3]
        ekv = sb("ekv", [P, KC, S])
        scan = sb("scan", [P, 8, KC, S])
        num1 = sb("num1", [P, KC, S])
        den1 = sb("den1", [P, KC, S])
        num2 = sb("num2", [P, 3, KC, S])
        den2 = sb("den2", [P, 3, KC, S])
        hid1 = sb("hid1", [P, KC, S])
        qk_hi = sb("qk_hi", [P, 2, KC, S], F32R)
        qk_lo = sb("qk_lo", [P, 2, KC, S], F32R)
        v_aug = sb("v_aug", [P, 2, QT, H, 32])
        fill = sb("fill", [P, S])
        q_st = sb("q_st", [P, SLOTS, HB, S], F32R)
        k_st = sb("k_st", [P, SLOTS, HB, S], F32R)
        mx = sb("mx", [P, 2, H, QT])
        nmax_hi = sb("nmax_hi", [H, KC, P], F32R)
        nmax_lo = sb("nmax_lo", [H, KC, P], F32R)
        prob = sb("prob", [P, PRING, QT, S])
        o_raw = sb("o_raw", [P, 4, S])
        rsum = sb("rsum", [P, QT, H])
        o_tok = sb("o_tok", [P, QT, H, HD])
        o_ch = sb("o_ch", [P, KC, S])
        x1 = x_sb
        ex2 = sb("ex2", [P, KC, S])
        hid2 = sb("hid2", [P, KC, S])
        hid_hi = sb("hid_hi", [P, KC, TOK], F32R)
        hid_lo = sb("hid_lo", [P, KC, TOK], F32R)
        gex = sb("gex", [P, QT, E])
        gden = sb("gden", [P, QT, E])
        score = sb("score", [P, QT, E])
        sbias = sb("sbias", [P, QT, G, EG])
        pmax = sb("pmax", [P, QT * G, 4])
        pmin = sb("pmin", [P, QT * G, 4])
        qmax = sb("qmax", [P, QT * G, 2])
        qmid = sb("qmid", [P, QT * G, 2])
        qlow = sb("qlow", [P, QT * G, 2])
        qsec = sb("qsec", [P, QT * G, 2])
        fmax = sb("fmax", [P, QT * G, 1])
        fmid = sb("fmid", [P, QT * G, 1])
        flow = sb("flow", [P, QT * G, 1])
        fsec = sb("fsec", [P, QT * G, 1])
        gsum = sb("gsum", [P, QT, G + 4])
        gtop = sb("gtop", [P, QT, 8])
        grep = sb("grep", [P, QT, G + 4])
        gpen = sb("gpen", [P, QT, G])
        masked = sb("masked", [P, QT, E + 2])
        etop = sb("etop", [P, QT, 8])
        erep = sb("erep", [P, QT, E + 2])
        wsel = sb("wsel", [P, QT, E])
        wsum = sb("wsum", [P, QT])
        wsum1 = sb("wsum1", [P, QT])
        wrec = sb("wrec", [P, QT])
        wful = sb("wful", [P, QT, E])
        wsplit = sb("wsplit", [P, QT, 2 * E])
        w_ch = sb("w_ch", [P, TOK], F32R)
        raw = clip[:, 0:2].rearrange("p k c s -> p k (c s)")
        t_hi = k_st[:, 2, 0:4].rearrange("p (k n) s -> p k (n s)", k=2)
        t_lo = k_st[:, 2, 4:8].rearrange("p (k n) s -> p k (n s)", k=2)
        sel = k_st[:, 0, 0].rearrange("p (k m) -> p k m", k=2)
        relu, sq, act = (scan[:, 2 * n:2 * n + 2].rearrange("p k c s -> p k (c s)") for n in range(3))
        act_hi, act_lo = (q_st[:, 2, 4 * n:4 * n + 4].rearrange("p (k n) s -> p k (n s)", k=2) for n in range(2))
        res = f_sb[:].rearrange("p c (k s) -> p c k s", k=2)

        ld_f = [sem(f"ld_f{b}") for b in range(B)]
        ld_x = [sem(f"ld_x{b}") for b in range(B)]
        ld_vec, ld_w, ld_gate = sem("ld_vec"), sem("ld_w"), sem("ld_gate")
        fill_ready, ld_fill = sem("fill_ready"), sem("ld_fill")
        st_qk = [sem(f"st_qk{w}") for w in range(2)]
        ld_stack = [sem(f"ld_stack{n}") for n in range(SLOTS)]
        ld_rows = [sem(f"ld_rows{n}") for n in range(SLOTS)]
        ld_raw = [sem(f"ld_raw{i}") for i in range(2)]
        st_out = sem("st_out")
        pool_const, dve_const, ident_ready, tile_no_ready = sem("pool_const"), sem("dve_const"), sem("ident_ready"), sem("tile_no_ready")
        tsum_ready, setup_exp, setup_step, decay_ready = sem("tsum_ready"), sem("setup_exp"), sem("setup_step"), sem("decay_ready")
        clip_ready, ex_ready, pool_pre, esum_ready = sem("clip_ready"), sem("ex_ready"), sem("pool_pre"), sem("esum_ready")
        fwd_ready, bwd_ready, numden_ready, den_ready = sem("fwd_ready"), sem("bwd_ready"), sem("numden_ready"), sem("den_ready")
        ln1_ready, lnsum1_ready, rec1_ready, hid1_ready = sem("ln1_ready"), sem("lnsum1_ready"), sem("rec1_ready"), sem("hid1_ready")
        misc_full = [sem(f"misc_full{i}") for i in range(2)]
        misc_free = [sem(f"misc_free{i}") for i in range(2)]
        qk_hi_ready, qk_lo_ready, v_ready = sem("qk_hi_ready"), sem("qk_lo_ready"), sem("v_ready")
        s_ready, max_ready, nmax_hi_ready, nmax_lo_ready = sem("s_ready"), sem("max_ready"), sem("nmax_hi_ready"), sem("nmax_lo_ready")
        t_ready, prob_ready, pv_ready, o_raw_ready = sem("t_ready"), sem("prob_ready"), sem("pv_ready"), sem("o_raw_ready")
        rsum_ready, o_tok_ready, o_ch_ready, x1_ready = sem("rsum_ready"), sem("o_tok_ready"), sem("o_ch_ready"), sem("x1_ready")
        clip2_ready, ex2_ready, lne2_ready, lnsum2_ready, rec2_ready = sem("clip2_ready"), sem("ex2_ready"), sem("lne2_ready"), sem("lnsum2_ready"), sem("rec2_ready")
        hid2_ready, hid_hi_ready, hid_lo_ready = sem("hid2_ready"), sem("hid_hi_ready"), sem("hid_lo_ready")
        gex_ready, route, wsplit_ready, w_ch_ready = sem("gex_ready"), sem("route"), sem("wsplit_ready"), sem("w_ch_ready")
        up_hi_ready, up_lo_ready, dn_hi_ready, dn_lo_ready = sem("up_hi_ready"), sem("up_lo_ready"), sem("dn_hi_ready"), sem("dn_lo_ready")
        sel_ready, h_ready, wb_ready, relu_ready = sem("sel_ready"), sem("h_ready"), sem("wb_ready"), sem("relu_ready")
        sq_ready, act_ready, act_hi_ready, act_lo_ready = sem("sq_ready"), sem("act_ready"), sem("act_hi_ready"), sem("act_lo_ready")
        down_done, res_ready = sem("down_done"), sem("res_ready")

        def slot(b, half):
            return (KC * b + half) % SLOTS

        def turn(b, half):
            return (KC * b + half) // SLOTS + 1

        def bank_s(n):
            return ps[:, n % 2, :].rearrange("p (t k) -> p t k", t=QT)

        def bank_t(n):
            return ps[:, 2 + n % 2, :].rearrange("p (t q) -> p t q", t=QT)

        def bank_o(n):
            return ps[:, 4 + n % 2, 0:S]

        jobs = [("q", 0), ("k", 0), ("v", 0)]
        for b in range(B):
            nxt, last = b + 1 < B, b > 0
            jobs += [("m", b, 0)]
            jobs += [("q", b + 1)] if nxt else []
            jobs += [("ot", b - 1, 0), ("ot", b - 1, 1)] if last else []
            jobs += [("k", b + 1)] if nxt else []
            jobs += [("oc", b - 1), ("proj", b - 1)] if last else []
            jobs += [("v", b + 1)] if nxt else []
            jobs += [("m", b, 1)]
            jobs += [("gate", b - 1)] if last else []
            jobs += [("wt", b - 2)] if b > 1 else []
        jobs += [("ot", B - 1, 0), ("ot", B - 1, 1), ("oc", B - 1), ("proj", B - 1), ("wt", B - 2),
                 ("gate", B - 1), ("wt", B - 1)]
        job_no = {job: n for n, job in enumerate(jobs)}

        def job_bank(job):
            return ps[:, 6 + job_no[job] % 2, :]

        def job_begin(eng, job):
            n = job_no[job]
            if n >= 2:
                eng.wait_ge(misc_free[n % 2], n // 2)

        def job_sem(job):
            return misc_full[job_no[job] % 2]

        def job_wait(eng, job):
            n = job_no[job]
            eng.wait_ge(misc_full[n % 2], n // 2 + 1)

        def job_free(job):
            return misc_free[job_no[job] % 2]

        def bank_h(half):
            return ps[:, half, :]

        def bank_w(half):
            return ps[:, 6 + half, :]

        def bank_acc(oc, half):
            return ps[:, 2 + 2 * oc + half, :]

        def tok(b):
            return slice(b * S, (b + 1) * S)

        block = ctx.enter_context(nc.Block())

        @block.sync
        def _(sp):
            sp.dma_start(vec[:], vecs).then_inc(ld_vec, 16)
            sp.dma_start(cond_sb[:], cond.partition_broadcast(P)).then_inc(ld_vec, 16)
            for b in range(B):
                sp.dma_start(f_sb[:, :, tok(b)], fT[:, :, tok(b)]).then_inc(ld_f[b], 16)
                sp.dma_start(x_sb[:, :, tok(b)], xT[:, :, tok(b)]).then_inc(ld_x[b], 16)
                if b == 0:
                    sp.dma_start(wi[:], w_in).then_inc(ld_w, 16)
                    sp.dma_start(bvb[:], bv.partition_broadcast(P)).then_inc(ld_w, 16)
                    sp.dma_start(wo[:], w_out).then_inc(ld_w, 16)
                    sp.wait_ge(fill_ready, 2)
                    for st, r0, r1 in ((q_st, STACK, MAXROW), (k_st, STACK, MAXROW), (k_st, MAXROW, MAXROW + 2)):
                        sp.dma_start(st[r0:r1].rearrange("p n h s -> p (n h) s").bitcast(F32),
                                     fill[r0:r1].unsqueeze(1).broadcast_to([r1 - r0, SLOTS * HB, S])).then_inc(ld_fill, 16)
            sp.dma_start(gw[:], gate_w).then_inc(ld_gate, 16)
            sp.dma_start(gbb[:], gate_bias.partition_broadcast(P)).then_inc(ld_gate, 16)

            def store_qk(b):
                for w in range(2):
                    for n, (part, ready) in enumerate(((qk_hi, qk_hi_ready), (qk_lo, qk_lo_ready))):
                        sp.wait_ge(ready, 4 * b + 2 * w + 2)
                        sp.dma_start(qk_dram[w, b, :, n].rearrange("t d (h s) -> (d h) t s", s=S),
                                     part[:, w].bitcast(F32)).then_inc(st_qk[w], 16)

            def load_stack(w, b, half):
                n = slot(b, half)
                sp.wait_ge(st_qk[w], 32 * (b + 1))
                if turn(b, half) > 1:
                    sp.wait_ge(t_ready, HB * (KC * b + half - SLOTS + 1))
                src = qk_dram[w, b, half]
                if w == 0:
                    loads = [(0, STACK, src.rearrange("n d s -> (n d) s"))]
                else:
                    loads = [(0, STACK // 2, src[0]), (STACK // 2, STACK, src[1])]
                for r0, r1, rows in loads:
                    sp.dma_start((q_st, k_st)[w][r0:r1, n].rearrange("p h s -> p (h s)").bitcast(F32),
                                 rows.unsqueeze(0).broadcast_to([2, (r1 - r0) // 2, HB * S])).then_inc(ld_stack[n], 16)

            def load_rows(b, half):
                for n, (src, ready) in enumerate(((nmax_hi, nmax_hi_ready), (nmax_lo, nmax_lo_ready))):
                    sp.wait_ge(ready, KC * b + half + 1)
                    dst = q_st[MAXROW + n:MAXROW + n + 1, slot(b, half)]
                    sp.dma_start(dst.rearrange("p h (t q) -> p (h t) q", t=QT).bitcast(F32),
                                 src[:, half, :].bitcast(F32)).then_inc(ld_rows[slot(b, half)], 16)

            store_qk(0)
            for half in range(KC):
                for w in range(2):
                    load_stack(w, 0, half)
            for b in range(B):
                load_rows(b, 0)
                if b + 1 < B:
                    store_qk(b + 1)
                    for w in range(2):
                        load_stack(w, b + 1, 0)
                if b + 1 == B:
                    sp.wait_ge(ex_ready, 4 * B)
                    sp.wait_ge(esum_ready, 4 * B)
                    for i in range(2):
                        sp.dma_start(raw[:, i, :], tiles[i]).then_inc(ld_raw[i], 16)
                load_rows(b, 1)
                if b + 1 < B:
                    for w in range(2):
                        load_stack(w, b + 1, 1)

            with sp.Fori(0, NT // 2 - 1) as i:
                for k in range(2):
                    sp.wait_ge(dn_hi_ready, 2 * i + k + 1)
                    sp.wait_ge(dn_lo_ready, 2 * i + k + 1)
                    sp.dma_start(raw[:, k, :], tiles[2 * i + k + 2]).then_inc(ld_raw[k], 16)
            for half in range(2):
                for oc in range(KC):
                    sp.wait_ge(res_ready, 2 * half + oc + 1)
                    sp.dma_start(out[:, oc, half * HT:(half + 1) * HT], res[:, oc, half, :]).then_inc(st_out, 16)
            sp.wait_ge(st_out, 16 * 2 * KC)

        @block.gpsimd
        def _(pool):
            g = nc.gpsimd
            g.memset(ident[:], 0.0).then_inc(pool_const, 1)
            pool.wait_ge(pool_const, 1)
            g.affine_select(out=ident[:], in_=ident[:], compare_op=ALU.not_equal, fill=1.0, base=0,
                            pattern=[[-1, P]], channel_multiplier=1).then_inc(ident_ready, 1)
            g.iota(sel_i[:], pattern=[[-1, 2], [0, E]], base=0, channel_multiplier=1).then_inc(pool_const, 1)
            g.iota(tile_i[:], pattern=[[2, TILES]], base=0, channel_multiplier=0).then_inc(pool_const, 1)
            pool.wait_ge(pool_const, 3)
            g.tensor_copy(selval[:], sel_i[:]).then_inc(pool_const, 1)
            g.tensor_copy(tile_no[:], tile_i[:]).then_inc(tile_no_ready, 1)

            def products(b):
                f = f_sb[:, :, tok(b)]
                pool.wait_ge(ld_f[b], 16)
                pool.wait_ge(ex_ready, 4 * b + 3)
                if b > 0:
                    pool.wait_ge(bwd_ready, 8 * b)
                g.tensor_tensor(ekv[:], ex[:, 0], f, ALU.mult).then_inc(pool_pre, 1)
                for n in range(2):
                    g.tensor_tensor(gk[:, n], gk[:, n], ex[:, 0], ALU.subtract).then_inc(pool_pre, 1)
                for n in range(2):
                    pool.wait_ge(pool_pre, 5 * b + 2 + n)
                    g.tensor_tensor(gkv[:, n], gk[:, n], f, ALU.mult).then_inc(pool_pre, 1)

            def sums(b, first, last):
                for i in range(first, last):
                    n = i % 2
                    if i < 2:
                        pool.wait_ge(pool_pre, 5 * b + 2 + n)
                        pool.wait_ge(fwd_ready, 8 * b + 2 * n + 2)
                        row, term = 2 + n, gk
                    else:
                        pool.wait_ge(pool_pre, 5 * b + 4 + n)
                        pool.wait_ge(fwd_ready, 8 * b + 4 + 2 * n + 2)
                        row, term = n, gkv
                    g.tensor_tensor(scan[:, row], scan[:, row], term[:, n], ALU.add).then_inc(esum_ready, 1)

            def add_logs1(b):
                pool.wait_ge(ln1_ready, 2 * (b + 1))
                g.tensor_tensor(den1[:], den1[:], ex[:, 3], ALU.add).then_inc(lnsum1_ready, 1)

            def add_logs2(b):
                pool.wait_ge(lne2_ready, 2 * (b + 1))
                g.tensor_tensor(den2[:, b % 3], den2[:, b % 3], ex2[:], ALU.add).then_inc(lnsum2_ready, 1)

            def split_hidden(b):
                pool.wait_ge(hid_hi_ready, b + 1)
                g.tensor_tensor(hid_lo[:, :, tok(b)], hid2[:], hid_hi[:, :, tok(b)].bitcast(F32),
                                ALU.subtract).then_inc(hid_lo_ready, 1)

            products(0)
            products(1)
            sums(1, 0, 4)
            add_logs1(1)
            for b in range(B):
                if b + 2 < B:
                    products(b + 2)
                    sums(b + 2, 0, 2)
                if b > 0:
                    add_logs2(b - 1)
                if b + 2 < B:
                    sums(b + 2, 2, 4)
                if b > 0:
                    split_hidden(b - 1)
                if b + 2 < B:
                    add_logs1(b + 2)

            def square(n, half):
                pool.wait_ge(relu_ready, n + 1)
                g.tensor_tensor(sq[:, half], relu[:, half], relu[:, half], ALU.mult).then_inc(sq_ready, 1)

            for n in range(2 * SHARED):
                k = n % SHARED
                if n >= SHARED:
                    pool.wait_ge(act_hi_ready, n - 1)
                    pool.wait_ge(act_lo_ready, n - 1)
                square(n, k)
                pool.wait_ge(act_hi_ready, n + 1)
                g.tensor_tensor(act_lo[:, k], sq[:, k], act_hi[:, k].bitcast(F32), ALU.subtract).then_inc(act_lo_ready, 1)
            for half in range(2):
                pool.wait_ge(act_lo_ready, 2 * (SHARED - 1) + half + 1)
                pool.wait_ge(act_hi_ready, 2 * (SHARED - 1) + half + 1)
                square(2 * SHARED + half, half)
            with pool.Fori(1, TILES) as t:
                for half in range(2):
                    pool.wait_ge(act_ready, 2 * (t - 1) + half + 1)
                    square(2 * (t + SHARED) + half, half)

        @block.scalar
        def _(sc):
            a = nc.scalar
            a.preload_act_table_set("natural_log_exp_and_others")
            sc.wait_ge(ld_vec, 32)
            for n, v in enumerate((V_W1, V_W2)):
                a.activation(dexp[:, n * KC:(n + 1) * KC], vec[:, v:v + KC], ACT.Exp).then_inc(setup_exp, 1)
            sc.wait_ge(setup_exp, 2)
            a.activation(dbase[:], dexp[:], ACT.Exp, scale=-1.0).then_inc(setup_exp, 1)
            sc.wait_ge(tsum_ready, 1)
            a.activation(tex[:], tsum[:], ACT.Exp, scale=-1.0).then_inc(setup_exp, 1)

            def exponentials(b):
                sc.wait_ge(clip_ready, 6 * (b + 1))
                if b > 0:
                    sc.wait_ge(esum_ready, 4 * b)
                    sc.wait_ge(bwd_ready, 8 * b)
                    sc.wait_ge(lnsum1_ready, b)
                for n in range(4):
                    a.activation(ex[:, n], clip[:, n], ACT.Exp, scale=1.0 if n < 3 else -1.0).then_inc(ex_ready, 1)
                sc.wait_ge(ex_ready, 4 * (b + 1))
                a.activation(ex[:, 3], ex[:, 3], ACT.Ln, bias=1.0).then_inc(ln1_ready, 1)

            def log_den(b):
                sc.wait_ge(den_ready, 2 * b + 1)
                a.activation(den1[:], den1[:], ACT.Ln).then_inc(ln1_ready, 1)

            def reciprocal1(b):
                sc.wait_ge(lnsum1_ready, b + 1)
                a.activation(den1[:], den1[:], ACT.Exp, scale=-1.0).then_inc(rec1_ready, 1)

            def evacuate_qk(b, w):
                sc.wait_ge(ld_vec, 32)
                if b > 0:
                    sc.wait_ge(st_qk[w], 32 * b)
                job = ("qk"[w], b)
                job_wait(sc, job)
                for t in range(KC):
                    u = (V_BQ, V_BK)[w] + t
                    a.activation(qk_hi[:, w, t], job_bank(job)[:, t * S:(t + 1) * S], ACT.Identity,
                                 bias=vec[:, u:u + 1]).then_inc(qk_hi_ready, 1)

            def negate_max(b, half):
                job = ("m", b, half)
                job_wait(sc, job)
                if b > 0:
                    sc.wait_ge(ld_rows[slot(b - 1, half)], 32 * turn(b - 1, half))
                a.activation(nmax_hi[:, half], job_bank(job)[0:H, 0:P], ACT.Copy, scale=-1.0).then_inc(nmax_hi_ready, 1)

            def probabilities(b, first, last):
                for h in range(first, last):
                    n = H * b + h
                    sc.wait_ge(t_ready, n + 1)
                    if n >= PRING:
                        sc.wait_ge(pv_ready, (n - PRING) // 4 + 1)
                    a.activation(prob[:, n % PRING], bank_t(n), ACT.Exp, scale=SCALE).then_inc(prob_ready, 1)

            def evacuate_o(b, grp):
                sc.wait_ge(pv_ready, 4 * b + grp + 1)
                if b > 0:
                    n = job_no[("ot", b - 1, 1)]
                    sc.wait_ge(misc_full[n % 2], n // 2 + 1)
                a.activation(o_raw[:, grp], bank_o(4 * b + grp), ACT.Copy).then_inc(o_raw_ready, 1)

            def evacuate_o_ch(b):
                job_wait(sc, ("oc", b))
                if b > 0:
                    n = job_no[("proj", b - 1)]
                    sc.wait_ge(misc_full[n % 2], n // 2 + 1)
                a.activation(o_ch[:], job_bank(("oc", b)).rearrange("p (t q) -> p t q", t=KC), ACT.Copy).then_inc(o_ch_ready, 1)
                sc.wait_ge(o_ch_ready, b + 1)
                sc.sem_inc(job_free(("oc", b)), 1)

            def second_exp(b):
                sc.wait_ge(clip2_ready, b + 1)
                a.activation(ex2[:], ex2[:], ACT.Exp, scale=-1.0).then_inc(ex2_ready, 1)
                sc.wait_ge(den_ready, 2 * b + 2)
                a.activation(den2[:, b % 3], den2[:, b % 3], ACT.Ln).then_inc(lne2_ready, 1)
                sc.wait_ge(ex2_ready, b + 1)
                a.activation(ex2[:], ex2[:], ACT.Ln, bias=1.0).then_inc(lne2_ready, 1)

            def second_rec(b):
                sc.wait_ge(lnsum2_ready, b + 1)
                a.activation(den2[:, b % 3], den2[:, b % 3], ACT.Exp, scale=-1.0).then_inc(rec2_ready, 1)

            def round_hidden(b):
                sc.wait_ge(hid2_ready, b + 1)
                a.activation(hid_hi[:, :, tok(b)], hid2[:], ACT.Copy).then_inc(hid_hi_ready, 1)

            def gate_exp(b):
                job = ("gate", b)
                job_wait(sc, job)
                if b > 0:
                    sc.wait_ge(wsplit_ready, 2 * b)
                a.activation(gex[:], job_bank(job)[:, 0:QT * E].rearrange("p (t e) -> p t e", t=QT), ACT.Exp,
                             scale=-1.0).then_inc(gex_ready, 1)
                sc.wait_ge(gex_ready, b + 1)
                sc.sem_inc(job_free(job), 1)

            def evacuate_w(b):
                job_wait(sc, ("wt", b))
                a.activation(w_ch[:, tok(b)], job_bank(("wt", b))[:, 0:S], ACT.Copy).then_inc(w_ch_ready, 1)
                sc.wait_ge(w_ch_ready, b + 1)
                sc.sem_inc(job_free(("wt", b)), 1)

            def split_up(k):
                sc.wait_ge(ld_raw[k], 16)
                a.activation(t_hi[:, k, 0:C], raw[:, k, 0:C], ACT.Copy).then_inc(up_hi_ready, 1)

            def split_down(k):
                a.activation(t_hi[:, k, C:2 * C], raw[:, k, C:2 * C], ACT.Copy).then_inc(dn_hi_ready, 1)

            def rectify(n, half):
                sc.wait_ge(h_ready, n + 1)
                a.activation(relu[:, half], bank_h(half), ACT.Relu).then_inc(relu_ready, 1)

            def round_act(n, half):
                sc.wait_ge(act_ready, n - 2 * SHARED + 1)
                a.activation(act_hi[:, half], act[:, half], ACT.Copy).then_inc(act_hi_ready, 1)

            def round_shared(n, half):
                sc.wait_ge(sq_ready, n + 1)
                a.activation(act_hi[:, half], sq[:, half], ACT.Copy).then_inc(act_hi_ready, 1)

            exponentials(0)
            log_den(0)
            reciprocal1(0)
            exponentials(1)
            evacuate_qk(0, 0)
            evacuate_qk(0, 1)
            log_den(1)
            reciprocal1(1)
            exponentials(2)
            for b in range(B):
                if b > 0:
                    probabilities(b - 1, HB, H - 1)
                negate_max(b, 0)
                if b > 0:
                    probabilities(b - 1, H - 1, H)
                    evacuate_o(b - 1, 2)
                    evacuate_o(b - 1, 3)
                if b + 1 < B:
                    evacuate_qk(b + 1, 0)
                probabilities(b, 0, 1)
                if b + 1 < B:
                    evacuate_qk(b + 1, 1)
                probabilities(b, 1, 2)
                if b > 0:
                    evacuate_o_ch(b - 1)
                probabilities(b, 2, 6)
                negate_max(b, 1)
                if b + 1 == B:
                    split_up(0)
                    split_up(1)
                if b > 0:
                    second_exp(b - 1)
                probabilities(b, 6, 7)
                if b > 0:
                    second_rec(b - 1)
                probabilities(b, 7, 8)
                if b + 2 < B:
                    log_den(b + 2)
                evacuate_o(b, 0)
                if b > 0:
                    round_hidden(b - 1)
                if b + 1 == B:
                    probabilities(b, HB, HB + 2)
                    rectify(0, 0)
                if b > 0:
                    gate_exp(b - 1)
                if b + 1 == B:
                    rectify(1, 1)
                if b + 2 < B:
                    reciprocal1(b + 2)
                evacuate_o(b, 1)
                if b > 1:
                    evacuate_w(b - 2)
                if b + 3 < B:
                    exponentials(b + 3)

            probabilities(B - 1, HB + 2, H)
            evacuate_o(B - 1, 2)
            split_down(0)
            evacuate_o(B - 1, 3)
            round_shared(0, 0)
            split_down(1)
            round_shared(1, 1)
            evacuate_o_ch(B - 1)
            evacuate_w(B - 2)
            second_exp(B - 1)
            second_rec(B - 1)
            round_hidden(B - 1)
            gate_exp(B - 1)
            for k in range(2):
                sc.wait_ge(sq_ready, k + 1)
                rectify(2 + k, k)
                sc.wait_ge(ld_raw[k], 32)
                a.activation(t_hi[:, k, 0:C], raw[:, k, 0:C], ACT.Copy).then_inc(up_hi_ready, 1)
            for k in range(2):
                sc.wait_ge(down_done, k + 1)
                round_shared(2 + k, k)
            evacuate_w(B - 1)

            def tile(t, k, split=True, up_wait=None):
                if split:
                    sc.wait_ge(ld_raw[1 - k], up_wait)
                    sc.wait_ge(h_ready, 2 * t)
                    a.activation(t_hi[:, 1 - k, 0:C], raw[:, 1 - k, 0:C], ACT.Copy).then_inc(up_hi_ready, 1)
                if isinstance(t, int) and t == SHARED:
                    sc.wait_ge(down_done, 2 * SHARED - 1)
                else:
                    sc.wait_ge(down_done, 2 * (t - 1))
                split_down(k)
                for half in range(2):
                    sc.wait_ge(sq_ready, 2 * (t - 1) + half + 1)
                    rectify(2 * t + half, half)
                for half in range(2):
                    sc.wait_ge(down_done, 2 * (t - 1) + half + 1)
                    round_act(2 * t + half, half)

            tile(2, 0, split=False)
            tile(3, 1, up_wait=48)
            with sc.Fori(2, NT // 2 - 1) as i:
                tile(2 * i, 0, up_wait=16 * i + 16)
                tile(2 * i + 1, 1, up_wait=16 * i + 32)
            tile(NT - 2, 0, up_wait=16 * (NT // 2))
            tile(NT - 1, 1, split=False)

        @block.vector
        def _(dve):
            v = nc.vector
            TT = v.tensor_tensor
            v.memset(fill[0:MAXROW], 0.0).then_inc(fill_ready, 1)
            v.memset(fill[MAXROW:P], 1.0).then_inc(fill_ready, 1)
            v.memset(v_aug[:, :, :, :, HD:32], 1.0).then_inc(dve_const, 1)
            v.memset(gsum[:, :, G:G + 4], NONE).then_inc(dve_const, 1)
            v.memset(masked[:, :, E:E + 2], NONE).then_inc(dve_const, 1)
            dve.wait_ge(pool_const, 4)
            v.tensor_scalar(selval[E:P, :], selval[E:P, :], float(-E), None, ALU.add).then_inc(dve_const, 1)

            def clips(b):
                dve.wait_ge(ld_f[b], 16)
                if b > 0:
                    dve.wait_ge(ex_ready, 4 * b)
                    dve.wait_ge(esum_ready, 4 * b)
                f = f_sb[:, :, tok(b)]
                v.tensor_scalar(clip[:, 0], f, 30.0, None, ALU.min).then_inc(clip_ready, 1)
                for n, u in enumerate((V_U1, V_U2)):
                    for c in range(KC):
                        v.tensor_scalar(clip[:, 1 + n, c], f[:, c], vec[:, u + c:u + c + 1], 30.0,
                                        ALU.add, ALU.min).then_inc(clip_ready, 1)
                dve.wait_ge(ld_x[b], 16)
                v.tensor_scalar(clip[:, 3], x_sb[:, :, tok(b)], -41.0, None, ALU.max).then_inc(clip_ready, 1)

            dve.wait_ge(ld_vec, 32)
            v.tensor_reduce(tsum[:], cond_sb[:], AX_X, ALU.add).then_inc(tsum_ready, 1)
            dve.wait_ge(setup_exp, 4)
            v.tensor_scalar(tden[:], tex[:], 1.0, None, ALU.add).then_inc(setup_step, 1)
            dve.wait_ge(setup_step, 1)
            v.reciprocal(tf[:], tden[:]).then_inc(setup_step, 1)
            dve.wait_ge(setup_step, 2)
            v.tensor_scalar(thalf[:], tf[:], 0.5, 0.5, ALU.mult, ALU.add).then_inc(setup_step, 1)
            v.tensor_scalar(cfac[:], tf[:], 0.2, 0.8, ALU.mult, ALU.add).then_inc(setup_step, 1)
            dve.wait_ge(setup_step, 4)
            for n in range(2 * KC):
                v.tensor_scalar(decay[:, n], thalf[:], dbase[:, n:n + 1], None, ALU.mult).then_inc(decay_ready, 1)

            clips(0)

            def scans(b, back, first, last):
                for i in range(first, last):
                    which, n, c = 1 - i // 4, i // 2 % 2, i % 2
                    if i == 0 and not back:
                        dve.wait_ge(decay_ready, 2 * KC)
                        if b > 0:
                            dve.wait_ge(numden_ready, 4 * b)
                        dve.wait_ge(ex_ready, 4 * b + 1)
                    if i == 4 and not back:
                        dve.wait_ge(pool_pre, 5 * b + 1)
                    src = (ekv[:, c], ex[:, 0, c])[which]
                    dst = scan[:, 4 * back + 2 * which + n, c]
                    if back:
                        src, dst = src[:, ::-1], dst[:, ::-1]
                    v.tensor_tensor_scan(dst, decay[:, n * KC + c, b:b + 1].broadcast_to([P, S]), src, 0.0,
                                         ALU.mult, ALU.add).then_inc((fwd_ready, bwd_ready)[back], 1)

            def num_den(b, which):
                if b > 0:
                    dve.wait_ge(hid1_ready, b)
                if b > 2:
                    dve.wait_ge(hid2_ready, b - 2)
                dst = ((num1[:], num2[:, b % 3]), (den1[:], den2[:, b % 3]))
                for n in range(2):
                    dve.wait_ge(esum_ready, 4 * b + 2 * (1 - which) + n + 1)
                    dve.wait_ge(bwd_ready, 8 * b + 4 * (1 - which) + 2 * n + 2)
                    row = 2 * which + n
                    TT(dst[which][n], scan[:, row], scan[:, 4 + row], ALU.add).then_inc(numden_ready, 1)
                if which == 1:
                    for n in range(2):
                        dve.wait_ge(numden_ready, 4 * b + 1 + n)
                        v.tensor_scalar(dst[1][n], dst[1][n], 1e-8, None, ALU.max).then_inc(den_ready, 1)

            def first_sums(which):
                for n in range(2):
                    dve.wait_ge(pool_pre, (4 if which == 0 else 2) + n)
                    dve.wait_ge(fwd_ready, 4 * (1 - which) + 2 * n + 2)
                    row = 2 * which + n
                    TT(scan[:, row], scan[:, row], (gkv, gk)[which][:, n], ALU.add).then_inc(esum_ready, 1)

            def first_logs():
                dve.wait_ge(ln1_ready, 2)
                TT(den1[:], den1[:], ex[:, 3], ALU.add).then_inc(lnsum1_ready, 1)

            def hidden1(b):
                dve.wait_ge(rec1_ready, b + 1)
                dve.wait_ge(numden_ready, 4 * b + 3)
                if b > 0:
                    job_wait(dve, ("k", b - 1))
                v.scalar_tensor_tensor(hid1[:], num1[:], cfac[:, b:b + 1], den1[:], ALU.mult,
                                       ALU.mult).then_inc(hid1_ready, 1)

            def split_qk(b, w):
                u = (V_BQ, V_BK)[w]
                job = ("qk"[w], b)
                dve.wait_ge(qk_hi_ready, 4 * b + 2 * w + 2)
                for t in range(KC):
                    v.scalar_tensor_tensor(qk_lo[:, w, t], job_bank(job)[:, t * S:(t + 1) * S],
                                           vec[:, u + t:u + t + 1], qk_hi[:, w, t].bitcast(F32), ALU.add,
                                           ALU.subtract).then_inc(qk_lo_ready, 1)
                dve.wait_ge(qk_lo_ready, 4 * b + 2 * w + 2)
                dve.sem_inc(job_free(job), 1)

            def add_v_bias(b):
                job = ("v", b)
                job_wait(dve, job)
                for t in range(QT):
                    if b > 1 and t == 0:
                        dve.wait_ge(pv_ready, 4 * (b - 1))
                    src = job_bank(job)[:, t * C:(t + 1) * C].rearrange("p (h d) -> p h d", d=HD)
                    TT(v_aug[:, b % 2, t, :, 0:HD], src, bvb[:].rearrange("p (h d) -> p h d", d=HD),
                       ALU.add).then_inc(v_ready, 1)
                dve.wait_ge(v_ready, QT * (b + 1))
                dve.sem_inc(job_free(job), 1)

            def maximum(b, h):
                n = H * b + h
                dve.wait_ge(s_ready, n + 1)
                if b > 1 and h == 0:
                    n2 = job_no[("m", b - 2, 1)]
                    dve.wait_ge(misc_full[n2 % 2], n2 // 2 + 1)
                v.tensor_reduce(mx[:, b % 2, h], bank_s(n), AX_X, ALU.max).then_inc(max_ready, 1)

            def low_max(b, half):
                job = ("m", b, half)
                dve.wait_ge(nmax_hi_ready, KC * b + half + 1)
                v.scalar_tensor_tensor(nmax_lo[:, half], job_bank(job)[0:H, 0:P], -1.0, nmax_hi[:, half].bitcast(F32),
                                       ALU.mult, ALU.subtract).then_inc(nmax_lo_ready, 1)
                dve.wait_ge(nmax_lo_ready, KC * b + half + 1)
                dve.sem_inc(job_free(job), 1)

            def normalise(b):
                for qt in range(QT):
                    job = ("ot", b, qt)
                    job_wait(dve, job)
                    src = job_bank(job).rearrange("p (h c) -> p h c", c=32)
                    if b > 0 and qt == 0:
                        n = job_no[("oc", b - 1)]
                        dve.wait_ge(misc_full[n % 2], n // 2 + 1)
                    v.reciprocal(rsum[:, qt], src[:, :, HD]).then_inc(rsum_ready, 1)
                    dve.wait_ge(rsum_ready, QT * b + qt + 1)
                    TT(o_tok[:, qt], src[:, :, 0:HD], rsum[:, qt].unsqueeze(2).broadcast_to([P, H, HD]),
                       ALU.mult).then_inc(o_tok_ready, 1)
                    dve.wait_ge(o_tok_ready, QT * b + qt + 1)
                    dve.sem_inc(job_free(job), 1)

            def residual(b):
                job = ("proj", b)
                job_wait(dve, job)
                for c in range(KC):
                    v.scalar_tensor_tensor(x1[:, c, tok(b)], job_bank(job)[:, c * S:(c + 1) * S],
                                           vec[:, V_BP + c:V_BP + c + 1], x_sb[:, c, tok(b)], ALU.add,
                                           ALU.add).then_inc(x1_ready, 1)
                dve.wait_ge(x1_ready, KC * (b + 1))
                dve.sem_inc(job_free(job), 1)
                if b > 0:
                    dve.wait_ge(lnsum2_ready, b)
                v.tensor_scalar(ex2[:], x1[:, :, tok(b)], -41.0, None, ALU.max).then_inc(clip2_ready, 1)

            def hidden2(b):
                dve.wait_ge(rec2_ready, b + 1)
                dve.wait_ge(numden_ready, 4 * b + 4)
                if b > 0:
                    dve.wait_ge(hid_hi_ready, b)
                    dve.wait_ge(hid_lo_ready, b)
                    n = job_no[("gate", b - 1)]
                    dve.wait_ge(misc_full[n % 2], n // 2 + 1)
                v.scalar_tensor_tensor(hid2[:], num2[:, b % 3], cfac[:, b:b + 1], den2[:, b % 3], ALU.mult,
                                       ALU.mult).then_inc(hid2_ready, 1)

            def router(b):
                count = [b * ROUTE_STEPS]

                def step(ins):
                    ins.then_inc(route, 1)
                    count[0] += 1

                def settled():
                    dve.wait_ge(route, count[0])

                if b == 0:
                    dve.wait_ge(ld_gate, 32)
                dve.wait_ge(gex_ready, b + 1)
                step(v.tensor_scalar(gden[:], gex[:], 1.0, None, ALU.add))
                yield
                settled()
                step(v.reciprocal(score[:], gden[:]))
                yield
                settled()
                for t in range(QT):
                    step(TT(sbias[:, t], score[:, t].rearrange("p (g e) -> p g e", g=G),
                            gbb[:].rearrange("p (g e) -> p g e", g=G), ALU.add))
                yield
                settled()
                pairs = sbias[:].rearrange("p t g (a c) -> p (t g) a c", c=2)
                step(TT(pmax[:], pairs[:, :, :, 0], pairs[:, :, :, 1], ALU.max))
                step(TT(pmin[:], pairs[:, :, :, 0], pairs[:, :, :, 1], ALU.min))
                yield
                for best, low, nbest, mid, nlow, nsec, w in ((pmax, pmin, qmax, qmid, qlow, qsec, 2),
                                                             (qmax, qsec, fmax, fmid, flow, fsec, 1)):
                    settled()
                    step(TT(nbest[:], best[:, :, 0:w], best[:, :, w:2 * w], ALU.max))
                    step(TT(mid[:], best[:, :, 0:w], best[:, :, w:2 * w], ALU.min))
                    step(TT(nlow[:], low[:, :, 0:w], low[:, :, w:2 * w], ALU.max))
                    yield
                    settled()
                    step(TT(nsec[:], mid[:], nlow[:], ALU.max))
                    yield
                settled()
                step(TT(gsum[:, :, 0:G], fmax[:, :, 0].rearrange("p (t g) -> p t g", t=QT),
                        fsec[:, :, 0].rearrange("p (t g) -> p t g", t=QT), ALU.add))
                yield
                settled()
                for t in range(QT):
                    step(v.max(gtop[:, t], gsum[:, t, 0:G]))
                yield
                settled()
                step(v.memset(gtop[:, :, GT:8], NONE))
                yield
                settled()
                for t in range(QT):
                    step(v.match_replace(grep[:, t], gtop[:, t], gsum[:, t], BIG))
                yield
                settled()
                step(v.tensor_scalar(gpen[:], grep[:, :, 0:G], BIG, -BIG, ALU.is_lt, ALU.mult))
                yield
                settled()
                for t in range(QT):
                    step(TT(masked[:, t, 0:E].rearrange("p (g e) -> p g e", g=G), sbias[:, t],
                            gpen[:, t].unsqueeze(2).broadcast_to([P, G, EG]), ALU.add))
                yield
                settled()
                for t in range(QT):
                    step(v.max(etop[:, t], masked[:, t, 0:E]))
                yield
                settled()
                step(v.memset(etop[:, :, TOPK:8], NONE))
                yield
                settled()
                for t in range(QT):
                    step(v.match_replace(erep[:, t], etop[:, t], masked[:, t], BIG))
                yield
                settled()
                step(v.scalar_tensor_tensor(wsel[:], erep[:, :, 0:E], BIG, score[:], ALU.is_ge, ALU.mult))
                yield
                settled()
                step(v.tensor_reduce(wsum[:], wsel[:], AX_X, ALU.add))
                yield
                settled()
                step(v.tensor_scalar(wsum1[:], wsum[:], 1e-20, None, ALU.add))
                yield
                settled()
                step(v.reciprocal(wrec[:], wsum1[:]))
                yield
                settled()
                for t in range(QT):
                    step(v.tensor_scalar(wful[:, t], wsel[:, t], wrec[:, t:t + 1], 2.5, ALU.mult, ALU.mult))
                yield
                assert count[0] == (b + 1) * ROUTE_STEPS, count[0]
                settled()
                if b > 0:
                    n = job_no[("wt", b - 1)]
                    dve.wait_ge(misc_full[n % 2], n // 2 + 1)
                v.tensor_copy(wsplit[:, :, 0:E].bitcast(F32R), wful[:]).then_inc(wsplit_ready, 1)
                yield
                dve.wait_ge(wsplit_ready, 2 * b + 1)
                TT(wsplit[:, :, E:2 * E].bitcast(F32R), wful[:], wsplit[:, :, 0:E], ALU.subtract).then_inc(wsplit_ready, 1)
                yield

            ROUTE_STEPS = 34

            def split_up(k):
                TT(t_lo[:, k, 0:C], raw[:, k, 0:C], t_hi[:, k, 0:C].bitcast(F32), ALU.subtract).then_inc(up_lo_ready, 1)

            def split_down(k):
                TT(t_lo[:, k, C:2 * C], raw[:, k, C:2 * C], t_hi[:, k, C:2 * C].bitcast(F32),
                   ALU.subtract).then_inc(dn_lo_ready, 1)

            scans(0, 0, 0, 4)
            scans(0, 1, 0, 4)
            scans(0, 0, 4, 8)
            first_sums(1)
            num_den(0, 1)
            scans(0, 1, 4, 8)
            first_sums(0)
            num_den(0, 0)
            first_logs()
            hidden1(0)
            clips(1)
            scans(1, 0, 0, 8)
            dve.wait_ge(ld_w, 48)
            split_qk(0, 0)
            scans(1, 1, 0, 4)
            split_qk(0, 1)
            scans(1, 1, 4, 8)
            add_v_bias(0)
            num_den(1, 1)
            clips(2)
            num_den(1, 0)
            route_last = iter(())
            for b in range(B):
                nxt, nxt2 = b + 1 < B, b + 2 < B
                for h in range(HB):
                    maximum(b, h)
                    next(route_last, None)
                    if nxt and h == 5:
                        hidden1(b + 1)
                low_max(b, 0)
                maximum(b, HB)
                maximum(b, HB + 1)
                maximum(b, HB + 2)
                next(route_last, None)
                maximum(b, HB + 3)
                next(route_last, None)
                if nxt2:
                    scans(b + 2, 0, 0, 4)
                else:
                    next(route_last, None)
                    next(route_last, None)
                if nxt:
                    split_qk(b + 1, 0)
                if b > 0:
                    normalise(b - 1)
                maximum(b, HB + 4)
                next(route_last, None)
                maximum(b, HB + 5)
                next(route_last, None)
                if nxt:
                    split_qk(b + 1, 1)
                if nxt2:
                    scans(b + 2, 0, 4, 6)
                maximum(b, HB + 6)
                next(route_last, None)
                maximum(b, HB + 7)
                next(route_last, None)
                if b > 0:
                    residual(b - 1)
                if nxt2:
                    scans(b + 2, 0, 6, 8)
                if nxt:
                    add_v_bias(b + 1)
                low_max(b, 1)
                if b + 1 == B:
                    for k in range(2):
                        dve.wait_ge(up_hi_ready, k + 1)
                        split_up(k)
                for _ in route_last:
                    pass
                if nxt2:
                    scans(b + 2, 1, 0, 6)
                if b > 0:
                    hidden2(b - 1)
                if nxt2:
                    scans(b + 2, 1, 6, 8)
                    num_den(b + 2, 1)
                    num_den(b + 2, 0)
                if b + 3 < B:
                    clips(b + 3)
                route_last = router(b - 1) if b > 0 else iter(())

            def select(t, k):
                v.tensor_scalar(sel[:, k], selval[:], tile_no[:, bass.ds(t, 1)], None, ALU.is_equal).then_inc(sel_ready, 1)

            for _ in route_last:
                pass
            dve.wait_ge(dn_hi_ready, 1)
            split_down(0)
            normalise(B - 1)
            dve.wait_ge(dn_hi_ready, 2)
            split_down(1)
            residual(B - 1)
            dve.wait_ge(lne2_ready, 2 * B)
            TT(den2[:, (B - 1) % 3], den2[:, (B - 1) % 3], ex2[:], ALU.add).then_inc(lnsum2_ready, 1)
            hidden2(B - 1)
            dve.wait_ge(hid_hi_ready, B)
            TT(hid_lo[:, :, tok(B - 1)], hid2[:], hid_hi[:, :, tok(B - 1)].bitcast(F32),
               ALU.subtract).then_inc(hid_lo_ready, 1)

            def gated(n, half):
                dve.wait_ge(sq_ready, n + 1)
                dve.wait_ge(wb_ready, n - 2 * SHARED + 1)
                dve.wait_ge(act_lo_ready, n - 1)
                TT(act[:, half], sq[:, half], bank_w(half), ALU.mult).then_inc(act_ready, 1)

            def low_act(n, half):
                dve.wait_ge(act_hi_ready, n + 1)
                TT(act_lo[:, half], act[:, half], act_hi[:, half].bitcast(F32), ALU.subtract).then_inc(act_lo_ready, 1)

            dve.wait_ge(tile_no_ready, 1)
            dve.wait_ge(dve_const, 4)
            route_last = router(B - 1)
            for _ in range(5):
                next(route_last, None)
            dve.wait_ge(up_hi_ready, 3)
            split_up(0)
            for _ in route_last:
                pass
            select(0, 0)
            dve.wait_ge(up_hi_ready, 4)
            split_up(1)

            def tile(t, k, split=True, pick=True):
                if split:
                    dve.wait_ge(up_hi_ready, t + 2)
                    split_up(1 - k)
                if pick:
                    if not isinstance(t, int) or t > SHARED:
                        dve.wait_ge(wb_ready, 2 * (t - SHARED))
                    select(t - SHARED + 1, 1 - k)
                dve.wait_ge(dn_hi_ready, t + 1)
                split_down(k)
                for half in range(2):
                    gated(2 * t + half, half)
                for half in range(2):
                    dve.wait_ge(down_done, 2 * (t - 1) + half + 1)
                    low_act(2 * t + half, half)

            tile(2, 0, split=False)
            tile(3, 1)
            with dve.Fori(2, NT // 2 - 1) as i:
                tile(2 * i, 0)
                tile(2 * i + 1, 1)
            tile(NT - 2, 0)
            tile(NT - 1, 1, split=False, pick=False)
            for half in range(2):
                dve.wait_ge(down_done, 2 * NT - 1 + half)
                for oc in range(KC):
                    TT(res[:, oc, half], bank_acc(oc, half), x1[:, oc, half * HT:(half + 1) * HT],
                       ALU.add).then_inc(res_ready, 1)

        @block.tensor
        def _(pe):
            mm = nc.tensor.matmul

            def project(b, name):
                pe.wait_ge(hid1_ready, b + 1)
                job = (name, b)
                job_begin(pe, job)
                w = "qkv".index(name) * C
                for t in range(KC):
                    for c in range(KC):
                        weights, tokens = wi[:, c, w + t * P:w + (t + 1) * P], hid1[:, c, :]
                        if name == "v":
                            weights, tokens = hid1[:, c, t * P:(t + 1) * P], wi[:, c, w:w + C]
                        last = mm(job_bank(job)[:, t * S:(t + 1) * S], weights, tokens, start=(c == 0),
                                  stop=(c == KC - 1))
                last.then_inc(job_sem(job), 1)

            def scores(b, h):
                n = H * b + h
                if h % HB == 0:
                    pe.wait_ge(ld_stack[slot(b, h // HB)], 48 * turn(b, h // HB))
                if n >= 2:
                    pe.wait_ge(max_ready, n - 1)
                for qt in range(QT):
                    last = mm(bank_s(n)[:, qt], q_st[0:MAXROW, slot(b, h // HB), h % HB, qt * P:(qt + 1) * P],
                              k_st[0:MAXROW, slot(b, h // HB), h % HB, :], start=True, stop=True)
                last.then_inc(s_ready, 1)

            def turn_max(b, half):
                job = ("m", b, half)
                job_begin(pe, job)
                pe.wait_ge(max_ready, H * b + HB * (half + 1))
                nc.tensor.transpose(job_bank(job)[0:H, 0:P],
                                    mx[:, b % 2, half * HB:(half + 1) * HB].rearrange("p h t -> p (h t)"),
                                    ident[:]).then_inc(job_sem(job), 1)

            def shifted_scores(b, h):
                n = H * b + h
                if h % HB == 0:
                    pe.wait_ge(ld_rows[slot(b, h // HB)], 32 * turn(b, h // HB))
                if n >= 2:
                    pe.wait_ge(prob_ready, n - 1)
                for kt in range(QT):
                    last = mm(bank_t(n)[:, kt], k_st[0:MAXROW + 2, slot(b, h // HB), h % HB, kt * P:(kt + 1) * P],
                              q_st[0:MAXROW + 2, slot(b, h // HB), h % HB, :], start=True, stop=True)
                last.then_inc(t_ready, 1)

            def values(b, grp):
                if 4 * b + grp > 1:
                    pe.wait_ge(o_raw_ready, 4 * b + grp - 1)
                pe.wait_ge(v_ready, QT * (b + 1))
                pe.wait_ge(prob_ready, H * b + 4 * grp + 4)
                for kt in range(QT):
                    for j in range(4):
                        h = 4 * grp + j
                        last = mm(bank_o(4 * b + grp)[32 * j:32 * j + 32, :], v_aug[:, b % 2, kt, h, :],
                                  prob[:, (H * b + h) % PRING, kt, :], start=(kt == 0), stop=(kt == QT - 1))
                last.then_inc(pv_ready, 1)

            def turn_out(b):
                pe.wait_ge(o_raw_ready, 4 * (b + 1))
                for qt in range(QT):
                    job = ("ot", b, qt)
                    job_begin(pe, job)
                    for grp in range(4):
                        last = nc.tensor.transpose(job_bank(job)[:, grp * P:(grp + 1) * P],
                                                   o_raw[:, grp, qt * P:(qt + 1) * P], ident[:])
                    last.then_inc(job_sem(job), 1)

            def turn_normalised(b):
                job = ("oc", b)
                job_begin(pe, job)
                pe.wait_ge(o_tok_ready, QT * (b + 1))
                for c in range(KC):
                    for qt in range(QT):
                        last = nc.tensor.transpose(job_bank(job)[:, c * S + qt * P:c * S + (qt + 1) * P],
                                                   o_tok[:, qt, c * HB:(c + 1) * HB].rearrange("p h d -> p (h d)"), ident[:])
                last.then_inc(job_sem(job), 1)

            def project_out(b):
                job = ("proj", b)
                job_begin(pe, job)
                pe.wait_ge(o_ch_ready, b + 1)
                for t in range(KC):
                    for c in range(KC):
                        last = mm(job_bank(job)[:, t * S:(t + 1) * S], wo[:, c, t * P:(t + 1) * P], o_ch[:, c, :],
                                  start=(c == 0), stop=(c == KC - 1))
                last.then_inc(job_sem(job), 1)

            def gate(b):
                job = ("gate", b)
                job_begin(pe, job)
                pe.wait_ge(ld_gate, 32)
                pe.wait_ge(hid2_ready, b + 1)
                for t in range(QT):
                    for c in range(KC):
                        last = mm(job_bank(job)[:, t * E:(t + 1) * E], hid2[:, c, t * P:(t + 1) * P], gw[:, c, :],
                                  start=(c == 0), stop=(c == KC - 1))
                last.then_inc(job_sem(job), 1)

            def turn_weights(b):
                job = ("wt", b)
                job_begin(pe, job)
                pe.wait_ge(wsplit_ready, 2 * (b + 1))
                for t in range(QT):
                    last = nc.tensor.transpose(job_bank(job)[:, t * P:(t + 1) * P], wsplit[:, t], ident[:])
                last.then_inc(job_sem(job), 1)

            pe.wait_ge(ld_w, 48)
            for name in "qkv":
                project(0, name)
            pe.wait_ge(ident_ready, 1)
            pe.wait_ge(dve_const, 1)
            pe.wait_ge(ld_fill, 48)
            def second_half(b):
                for h in range(HB):
                    if b > 0:
                        shifted_scores(b - 1, HB + h)
                    if h + 2 < HB:
                        scores(b, h + 2)
                    if h == HB - 2:
                        turn_max(b, 0)
                        scores(b, HB)
                        scores(b, HB + 1)
                if b > 0:
                    values(b - 1, 2)
                scores(b, HB + 2)
                scores(b, HB + 3)
                if b > 0:
                    values(b - 1, 3)

            def up(k, half, slot, parts=(0, 1)):
                cols = slice(parts[0] * S, (parts[-1] + 1) * S)
                for c in range(KC):
                    w_hi, w_lo = (w[:, k, c * P:(c + 1) * P] for w in (t_hi, t_lo))
                    x_hi, x_lo = (x[:, c, half * HT:(half + 1) * HT][:, cols] for x in (hid_hi, hid_lo))
                    mm(bank_h(slot)[:, cols], w_hi, x_hi, start=(c == 0), stop=False)
                    mm(bank_h(slot)[:, cols], w_hi, x_lo, start=False, stop=False)
                    last = mm(bank_h(slot)[:, cols], w_lo, x_hi, start=False, stop=(c == KC - 1))
                if parts[-1] == 1:
                    last.then_inc(h_ready, 1)

            def shared_up(n, parts=(0, 1)):
                if parts[0] == 0:
                    pe.wait_ge(up_lo_ready, n % 2 + 1)
                    if n >= 2:
                        pe.wait_ge(relu_ready, n - 1)
                up(n % 2, n // 2, n % 2, parts)

            def down(k, half, slot, first=False, final=False):
                for oc in range(KC):
                    w_hi, w_lo = (w[:, k, C + oc * P:C + (oc + 1) * P] for w in (t_hi, t_lo))
                    acc = bank_acc(oc, half)
                    mm(acc, w_hi, act_hi[:, slot], start=first, stop=False, skip_group_check=True)
                    mm(acc, w_hi, act_lo[:, slot], start=False, stop=False, skip_group_check=True)
                    last = mm(acc, w_lo, act_hi[:, slot], start=False, stop=final, skip_group_check=True)
                last.then_inc(down_done, 1)

            def shared_down(n):
                pe.wait_ge(dn_lo_ready, n % 2 + 1)
                pe.wait_ge(act_lo_ready, n + 1)
                down(n % 2, n // 2, n % 2, first=(n % 2 == 0))

            scores(0, 0)
            scores(0, 1)
            for b in range(B):
                second_half(b)
                if b + 1 < B:
                    project(b + 1, "q")
                if b > 0:
                    turn_out(b - 1)
                scores(b, HB + 4)
                scores(b, HB + 5)
                shifted_scores(b, 0)
                if b + 1 < B:
                    project(b + 1, "k")
                shifted_scores(b, 1)
                if b > 0:
                    turn_normalised(b - 1)
                scores(b, HB + 6)
                scores(b, HB + 7)
                shifted_scores(b, 2)
                shifted_scores(b, 3)
                if b > 0:
                    project_out(b - 1)
                shifted_scores(b, 4)
                if b + 1 < B:
                    project(b + 1, "v")
                shifted_scores(b, 5)
                turn_max(b, 1)
                shifted_scores(b, 6)
                shifted_scores(b, 7)
                values(b, 0)
                if b + 1 < B:
                    scores(b + 1, 0)
                    scores(b + 1, 1)
                else:
                    pe.wait_ge(hid_lo_ready, 2)
                    pe.wait_ge(hid_hi_ready, 2)
                    pe.wait_ge(max_ready, H * B)
                    shared_up(0)
                    shared_up(1)
                    shifted_scores(b, HB)
                    shifted_scores(b, HB + 1)
                if b > 0:
                    gate(b - 1)
                values(b, 1)
                if b > 1:
                    turn_weights(b - 2)
            for h in range(HB + 2, H):
                shifted_scores(B - 1, h)
            values(B - 1, 2)
            values(B - 1, 3)
            turn_out(B - 1)
            shared_down(0)
            turn_normalised(B - 1)
            project_out(B - 1)
            turn_weights(B - 2)
            shared_down(1)

            def spread(k, half):
                mm(bank_w(half), sel[:, k], w_ch[:, half * HT:(half + 1) * HT], start=True,
                   stop=True).then_inc(wb_ready, 1)

            def step(t, k):
                pe.wait_ge(up_lo_ready, t + 1)
                for half in range(2):
                    pe.wait_ge(relu_ready, 2 * (t - 1) + half + 1)
                    up(k, half, half)
                    if half == 0:
                        pe.wait_ge(sel_ready, t - SHARED + 1)
                    pe.wait_ge(act_ready, 2 * (t - SHARED - 1) + half + 1)
                    spread(k, half)
                pe.wait_ge(dn_lo_ready, t)
                for half in range(2):
                    pe.wait_ge(act_lo_ready, 2 * (t - 1) + half + 1)
                    down(1 - k, half, half)

            pe.wait_ge(hid_lo_ready, B - 1)
            pe.wait_ge(hid_hi_ready, B - 1)
            shared_up(2, (0,))
            shared_up(3, (0,))
            gate(B - 1)
            pe.wait_ge(hid_lo_ready, B)
            pe.wait_ge(hid_hi_ready, B)
            shared_up(2, (1,))
            shared_up(3, (1,))
            pe.wait_ge(up_lo_ready, SHARED + 1)
            pe.wait_ge(relu_ready, 3)
            up(0, 0, 0)
            shared_down(2)
            pe.wait_ge(relu_ready, 4)
            up(0, 1, 1)
            turn_weights(B - 1)
            shared_down(3)
            pe.wait_ge(w_ch_ready, B)
            pe.wait_ge(sel_ready, 1)
            for half in range(2):
                spread(0, half)
            step(3, 1)
            with pe.Fori(2, NT // 2) as i:
                step(2 * i, 0)
                step(2 * i + 1, 1)
            pe.wait_ge(dn_lo_ready, NT)
            for half in range(2):
                pe.wait_ge(act_lo_ready, 2 * (NT - 1) + half + 1)
                down(1, half, half, final=True)


def kernel(**inputs):
    import numpy as np
    import concourse.bacc as bacc
    from concourse.bass_utils import run_bass_kernel_spmd

    def arr(name):
        return np.asarray(inputs[name])

    def chunks(a):
        return np.ascontiguousarray(a.reshape(KC, P, -1).transpose(1, 0, 2))

    x, f = arr("x"), arr("fside_BxSxS_0")
    wqkv = arr("L0_attn_Wqkv").reshape(KC, HB, 3, HD, C)
    bqkv = arr("L0_attn_bqkv").reshape(KC, HB, 3, HD)
    wqkv = np.concatenate([wqkv[:, :, 0:2].transpose(2, 0, 3, 1, 4).reshape(2 * C, C), wqkv[:, :, 2].reshape(C, C)])
    bqkv = np.concatenate([bqkv[:, :, 0:2].transpose(2, 0, 3, 1).reshape(2, C), bqkv[:, :, 2].reshape(1, C)])
    cols = [arr("L0_cond_w"), arr("L0_cond_u"), arr("L0_cond2_w"), arr("L0_cond2_u"), bqkv[0], bqkv[1],
            arr("L0_attn_bproj")]
    up = np.concatenate([arr("L0_ffn_shared_up"), arr("L0_ffn_w1").reshape(E * I, C)])
    down = np.concatenate([arr("L0_ffn_shared_down").T, arr("L0_ffn_w2").transpose(0, 2, 1).reshape(E * I, C)])
    up = up.reshape(NT, P, KC, P).transpose(0, 3, 2, 1).reshape(NT, P, C)
    arrays = {
        "xT": chunks(x.reshape(TOK, C).T),
        "fT": chunks(f.reshape(TOK, C).T),
        "cond": arr("cond_512"),
        "vecs": np.concatenate([v.reshape(KC, P).T for v in cols], axis=1),
        "w_in": chunks(wqkv.T),
        "w_out": chunks(arr("L0_attn_Wproj").T),
        "gate_w": chunks(arr("L0_ffn_gate_w").T),
        "bv": bqkv[2],
        "gate_bias": arr("L0_ffn_gate_bias"),
        "tiles": np.concatenate([up, down.reshape(NT, P, C)], axis=2),
    }
    arrays = {f"in_{n}": np.ascontiguousarray(a) for n, a in arrays.items()}
    nc = bacc.Bacc("TRN2", target_bir_lowering=False, num_devices=1)
    args = [nc.dram_tensor(n, a.shape, mybir.dt.from_np(a.dtype), kind="ExternalInput").ap() for n, a in arrays.items()]
    out = nc.dram_tensor("out", (P, KC, TOK), F32, kind="ExternalOutput").ap()
    bass_adaln_attn_ffn(nc, *args, out)
    r = run_bass_kernel_spmd(nc, [arrays], core_ids=[0])
    y = r.results[0]["out"]
    return np.ascontiguousarray(y.transpose(2, 1, 0).reshape(B, S, C))
```
